# Optimizing a Trainium2 kernel written in Bass

```python
import numpy as np
import jax
import jax.numpy as jnp

def _softmax(x, axis=-1):
    return jax.nn.softmax(x, axis=axis)

def _gelu(x):
    return jax.nn.gelu(x, approximate=True)

def _silu(x):
    return jax.nn.silu(x)

def _sigmoid(x):
    return jax.nn.sigmoid(x)

def _layernorm(x, axis=-1, eps=1e-05):
    m = jnp.mean(x, axis=axis, keepdims=True)
    v = jnp.var(x, axis=axis, keepdims=True)
    return (x - m) / jnp.sqrt(v + eps)

def _scatter_add(tgt, idx, src, axis=0):
    return tgt.at[idx].add(src)

def _segment_sum(src, seg, n):
    return jax.ops.segment_sum(src, seg, n)
kernel_name = 'mk_dlrm_tower_d1_rec_r8_e086f3'

def setup_inputs(seed: int=0):
    np.random.seed(seed)
    _w = jnp.asarray

    def _rec_inputs():
        import jax
        import jax.numpy as jnp
        _tk = jax.random.key(seed)
        dense_ctx = jax.random.normal(jax.random.fold_in(_tk, 190), (512, 16), jnp.float32)
        ids = jnp.stack([jax.random.randint(jax.random.fold_in(_tk, 200 + f), (512,), 0, v, jnp.int32) for f, v in enumerate([125000, 12500, 12500, 12500, 1000, 12500, 1000, 12500, 125000, 1250, 1000, 12500, 1250, 1250, 1250, 125000, 1250, 1250, 1000, 1250, 1000, 12500, 12500, 1250, 1000, 1250, 12500, 1000, 1000, 12500, 12500, 1250, 12500, 1000, 12500, 1000, 12500, 125000, 1250])], axis=1)
        tbl_0 = 0.05 * jax.random.normal(jax.random.fold_in(_tk, 500 + 0), (125000, 16), jnp.float32)
        tbl_1 = 0.05 * jax.random.normal(jax.random.fold_in(_tk, 500 + 1), (12500, 16), jnp.float32)
        tbl_2 = 0.05 * jax.random.normal(jax.random.fold_in(_tk, 500 + 2), (12500, 16), jnp.float32)
        tbl_3 = 0.05 * jax.random.normal(jax.random.fold_in(_tk, 500 + 3), (12500, 16), jnp.float32)
        tbl_4 = 0.05 * jax.random.normal(jax.random.fold_in(_tk, 500 + 4), (1000, 16), jnp.float32)
        tbl_5 = 0.05 * jax.random.normal(jax.random.fold_in(_tk, 500 + 5), (12500, 16), jnp.float32)
        tbl_6 = 0.05 * jax.random.normal(jax.random.fold_in(_tk, 500 + 6), (1000, 16), jnp.float32)
        tbl_7 = 0.05 * jax.random.normal(jax.random.fold_in(_tk, 500 + 7), (12500, 16), jnp.float32)
        tbl_8 = 0.05 * jax.random.normal(jax.random.fold_in(_tk, 500 + 8), (125000, 16), jnp.float32)
        tbl_9 = 0.05 * jax.random.normal(jax.random.fold_in(_tk, 500 + 9), (1250, 16), jnp.float32)
        tbl_10 = 0.05 * jax.random.normal(jax.random.fold_in(_tk, 500 + 10), (1000, 16), jnp.float32)
        tbl_11 = 0.05 * jax.random.normal(jax.random.fold_in(_tk, 500 + 11), (12500, 16), jnp.float32)
        tbl_12 = 0.05 * jax.random.normal(jax.random.fold_in(_tk, 500 + 12), (1250, 16), jnp.float32)
        tbl_13 = 0.05 * jax.random.normal(jax.random.fold_in(_tk, 500 + 13), (1250, 16), jnp.float32)
        tbl_14 = 0.05 * jax.random.normal(jax.random.fold_in(_tk, 500 + 14), (1250, 16), jnp.float32)
        tbl_15 = 0.05 * jax.random.normal(jax.random.fold_in(_tk, 500 + 15), (125000, 16), jnp.float32)
        tbl_16 = 0.05 * jax.random.normal(jax.random.fold_in(_tk, 500 + 16), (1250, 16), jnp.float32)
        tbl_17 = 0.05 * jax.random.normal(jax.random.fold_in(_tk, 500 + 17), (1250, 16), jnp.float32)
        tbl_18 = 0.05 * jax.random.normal(jax.random.fold_in(_tk, 500 + 18), (1000, 16), jnp.float32)
        tbl_19 = 0.05 * jax.random.normal(jax.random.fold_in(_tk, 500 + 19), (1250, 16), jnp.float32)
        tbl_20 = 0.05 * jax.random.normal(jax.random.fold_in(_tk, 500 + 20), (1000, 16), jnp.float32)
        tbl_21 = 0.05 * jax.random.normal(jax.random.fold_in(_tk, 500 + 21), (12500, 16), jnp.float32)
        tbl_22 = 0.05 * jax.random.normal(jax.random.fold_in(_tk, 500 + 22), (12500, 16), jnp.float32)
        tbl_23 = 0.05 * jax.random.normal(jax.random.fold_in(_tk, 500 + 23), (1250, 16), jnp.float32)
        tbl_24 = 0.05 * jax.random.normal(jax.random.fold_in(_tk, 500 + 24), (1000, 16), jnp.float32)
        tbl_25 = 0.05 * jax.random.normal(jax.random.fold_in(_tk, 500 + 25), (1250, 16), jnp.float32)
        tbl_26 = 0.05 * jax.random.normal(jax.random.fold_in(_tk, 500 + 26), (12500, 16), jnp.float32)
        tbl_27 = 0.05 * jax.random.normal(jax.random.fold_in(_tk, 500 + 27), (1000, 16), jnp.float32)
        tbl_28 = 0.05 * jax.random.normal(jax.random.fold_in(_tk, 500 + 28), (1000, 16), jnp.float32)
        tbl_29 = 0.05 * jax.random.normal(jax.random.fold_in(_tk, 500 + 29), (12500, 16), jnp.float32)
        tbl_30 = 0.05 * jax.random.normal(jax.random.fold_in(_tk, 500 + 30), (12500, 16), jnp.float32)
        tbl_31 = 0.05 * jax.random.normal(jax.random.fold_in(_tk, 500 + 31), (1250, 16), jnp.float32)
        tbl_32 = 0.05 * jax.random.normal(jax.random.fold_in(_tk, 500 + 32), (12500, 16), jnp.float32)
        tbl_33 = 0.05 * jax.random.normal(jax.random.fold_in(_tk, 500 + 33), (1000, 16), jnp.float32)
        tbl_34 = 0.05 * jax.random.normal(jax.random.fold_in(_tk, 500 + 34), (12500, 16), jnp.float32)
        tbl_35 = 0.05 * jax.random.normal(jax.random.fold_in(_tk, 500 + 35), (1000, 16), jnp.float32)
        tbl_36 = 0.05 * jax.random.normal(jax.random.fold_in(_tk, 500 + 36), (12500, 16), jnp.float32)
        tbl_37 = 0.05 * jax.random.normal(jax.random.fold_in(_tk, 500 + 37), (125000, 16), jnp.float32)
        tbl_38 = 0.05 * jax.random.normal(jax.random.fold_in(_tk, 500 + 38), (1250, 16), jnp.float32)
        _rk = jax.random.fold_in(_tk, 7)
        W_top1 = 0.05 * jax.random.normal(jax.random.fold_in(_tk, 801), (400, 512), jnp.float32)
        W_top2 = 0.0441942 * jax.random.normal(jax.random.fold_in(_tk, 802), (512, 256), jnp.float32)
        W_top3 = 0.0625 * jax.random.normal(jax.random.fold_in(_tk, 803), (256, 1), jnp.float32)
        b_top1 = jnp.zeros((512,), jnp.float32)
        b_top2 = jnp.zeros((256,), jnp.float32)
        return (dense_ctx, ids, tbl_0, tbl_1, tbl_2, tbl_3, tbl_4, tbl_5, tbl_6, tbl_7, tbl_8, tbl_9, tbl_10, tbl_11, tbl_12, tbl_13, tbl_14, tbl_15, tbl_16, tbl_17, tbl_18, tbl_19, tbl_20, tbl_21, tbl_22, tbl_23, tbl_24, tbl_25, tbl_26, tbl_27, tbl_28, tbl_29, tbl_30, tbl_31, tbl_32, tbl_33, tbl_34, tbl_35, tbl_36, tbl_37, tbl_38, W_top1, b_top1, W_top2, b_top2, W_top3)
    dense_ctx, ids, tbl_0, tbl_1, tbl_2, tbl_3, tbl_4, tbl_5, tbl_6, tbl_7, tbl_8, tbl_9, tbl_10, tbl_11, tbl_12, tbl_13, tbl_14, tbl_15, tbl_16, tbl_17, tbl_18, tbl_19, tbl_20, tbl_21, tbl_22, tbl_23, tbl_24, tbl_25, tbl_26, tbl_27, tbl_28, tbl_29, tbl_30, tbl_31, tbl_32, tbl_33, tbl_34, tbl_35, tbl_36, tbl_37, tbl_38, W_top1, b_top1, W_top2, b_top2, W_top3 = _rec_inputs()

    def _L0_rec_setup():
        import jax, jax.numpy as jnp
        import numpy as np
        B, F0, D = (256, 39, 16)
        CROSS = [128, 128, 128]
        key = jax.random.key(seed)
        k0, k1, k2, k3 = jax.random.split(key, 4)
        inputs = jax.random.normal(k0, (B, F0, D), dtype=jnp.float32)
        f0 = jax.random.normal(k1, (F0 * F0, CROSS[0]), dtype=jnp.float32) * 0.05
        f1 = jax.random.normal(k2, (CROSS[0] * F0, CROSS[1]), dtype=jnp.float32) * 0.05
        f2 = jax.random.normal(k3, (CROSS[1] * F0, CROSS[2]), dtype=jnp.float32) * 0.05
        return {'inputs': inputs, 'f0': f0, 'f1': f1, 'f2': f2}
    _L0_rec_all = _L0_rec_setup()
    _L0_rec_in = {k: v for k, v in _L0_rec_all.items() if k in ('f0', 'f1', 'f2')}
    del _L0_rec_all
    return {'dense_ctx': dense_ctx, 'ids': ids, 'tbl_0': tbl_0, 'tbl_1': tbl_1, 'tbl_2': tbl_2, 'tbl_3': tbl_3, 'tbl_4': tbl_4, 'tbl_5': tbl_5, 'tbl_6': tbl_6, 'tbl_7': tbl_7, 'tbl_8': tbl_8, 'tbl_9': tbl_9, 'tbl_10': tbl_10, 'tbl_11': tbl_11, 'tbl_12': tbl_12, 'tbl_13': tbl_13, 'tbl_14': tbl_14, 'tbl_15': tbl_15, 'tbl_16': tbl_16, 'tbl_17': tbl_17, 'tbl_18': tbl_18, 'tbl_19': tbl_19, 'tbl_20': tbl_20, 'tbl_21': tbl_21, 'tbl_22': tbl_22, 'tbl_23': tbl_23, 'tbl_24': tbl_24, 'tbl_25': tbl_25, 'tbl_26': tbl_26, 'tbl_27': tbl_27, 'tbl_28': tbl_28, 'tbl_29': tbl_29, 'tbl_30': tbl_30, 'tbl_31': tbl_31, 'tbl_32': tbl_32, 'tbl_33': tbl_33, 'tbl_34': tbl_34, 'tbl_35': tbl_35, 'tbl_36': tbl_36, 'tbl_37': tbl_37, 'tbl_38': tbl_38, 'W_top1': W_top1, 'b_top1': b_top1, 'W_top2': W_top2, 'b_top2': b_top2, 'W_top3': W_top3, 'L0_rec_f0': _L0_rec_in['f0'], 'L0_rec_f1': _L0_rec_in['f1'], 'L0_rec_f2': _L0_rec_in['f2']}

def reference(dense_ctx, ids, tbl_0, tbl_1, tbl_2, tbl_3, tbl_4, tbl_5, tbl_6, tbl_7, tbl_8, tbl_9, tbl_10, tbl_11, tbl_12, tbl_13, tbl_14, tbl_15, tbl_16, tbl_17, tbl_18, tbl_19, tbl_20, tbl_21, tbl_22, tbl_23, tbl_24, tbl_25, tbl_26, tbl_27, tbl_28, tbl_29, tbl_30, tbl_31, tbl_32, tbl_33, tbl_34, tbl_35, tbl_36, tbl_37, tbl_38, W_top1, b_top1, W_top2, b_top2, W_top3, L0_rec_f0, L0_rec_f1, L0_rec_f2):
    import jax
    import jax.numpy as jnp

    def _L0_rec_ref(inputs, f0, f1, f2):
        import jax, jax.numpy as jnp
        import numpy as np
        B, F0, D = (256, 39, 16)
        CROSS = [128, 128, 128]
        filters = [f0, f1, f2]
        x0 = inputs
        xk = inputs
        outs = []
        for W in filters:
            b, f, d = x0.shape
            g = xk.shape[1]
            z = jnp.einsum('bfd,bgd->bfgd', x0, xk).reshape(b, f * g, d)
            cur = jnp.einsum('bpd,pm->bmd', z, W)
            outs.append(cur)
            xk = cur
        result = jnp.concatenate(outs, axis=1)
        return jnp.sum(result, axis=-1)
    e = jnp.stack([tbl_0[ids[:, 0]], tbl_1[ids[:, 1]], tbl_2[ids[:, 2]], tbl_3[ids[:, 3]], tbl_4[ids[:, 4]], tbl_5[ids[:, 5]], tbl_6[ids[:, 6]], tbl_7[ids[:, 7]], tbl_8[ids[:, 8]], tbl_9[ids[:, 9]], tbl_10[ids[:, 10]], tbl_11[ids[:, 11]], tbl_12[ids[:, 12]], tbl_13[ids[:, 13]], tbl_14[ids[:, 14]], tbl_15[ids[:, 15]], tbl_16[ids[:, 16]], tbl_17[ids[:, 17]], tbl_18[ids[:, 18]], tbl_19[ids[:, 19]], tbl_20[ids[:, 20]], tbl_21[ids[:, 21]], tbl_22[ids[:, 22]], tbl_23[ids[:, 23]], tbl_24[ids[:, 24]], tbl_25[ids[:, 25]], tbl_26[ids[:, 26]], tbl_27[ids[:, 27]], tbl_28[ids[:, 28]], tbl_29[ids[:, 29]], tbl_30[ids[:, 30]], tbl_31[ids[:, 31]], tbl_32[ids[:, 32]], tbl_33[ids[:, 33]], tbl_34[ids[:, 34]], tbl_35[ids[:, 35]], tbl_36[ids[:, 36]], tbl_37[ids[:, 37]], tbl_38[ids[:, 38]]], axis=1)
    z = _L0_rec_ref(e, L0_rec_f0, L0_rec_f1, L0_rec_f2)
    z = z.reshape(z.shape[0], -1)
    h = jnp.concatenate([z, dense_ctx], axis=1)
    h = jnp.maximum(h @ W_top1 + b_top1, 0.0)
    h = jnp.maximum(h @ W_top2 + b_top2, 0.0)
    y = h @ W_top3
    return y

_drawn_inputs = setup_inputs


def setup_inputs(seed=0):
    import zlib

    import numpy as np

    out = dict(_drawn_inputs(seed))
    spreads = {'b_top1': (0.0, 0.653), 'b_top2': (0.0, 0.271)}
    factors = {'tbl_0': 4.414,
     'tbl_1': 5.361,
     'tbl_2': 4.765,
     'tbl_3': 4.927,
     'tbl_4': 4.864,
     'tbl_5': 4.765,
     'tbl_6': 4.539,
     'tbl_7': 4.802,
     'tbl_8': 5.046,
     'tbl_9': 5.002,
     'tbl_10': 5.168,
     'tbl_11': 4.594,
     'tbl_12': 4.328,
     'tbl_13': 4.575,
     'tbl_14': 4.605,
     'tbl_15': 5.069,
     'tbl_16': 5.369,
     'tbl_17': 4.907,
     'tbl_18': 5.19,
     'tbl_19': 4.838,
     'tbl_20': 4.969,
     'tbl_21': 4.737,
     'tbl_22': 4.439,
     'tbl_23': 4.96,
     'tbl_24': 4.792,
     'tbl_25': 4.481,
     'tbl_26': 4.978,
     'tbl_27': 5.172,
     'tbl_28': 5.073,
     'tbl_29': 5.015,
     'tbl_30': 4.669,
     'tbl_31': 4.552,
     'tbl_32': 5.053,
     'tbl_33': 5.137,
     'tbl_34': 4.481,
     'tbl_35': 5.038,
     'tbl_36': 4.681,
     'tbl_37': 5.048,
     'tbl_38': 4.91,
     'L0_rec_f1': 5.41,
     'L0_rec_f2': 8.0}
    for name, (base, spread) in spreads.items():
        noise = np.random.default_rng([zlib.crc32(name.encode()), seed]).standard_normal(out[name].shape)
        drawn = base * np.exp(spread * noise) if base else spread * noise
        out[name] = jnp.asarray(drawn.astype(out[name].dtype))
    for name, factor in factors.items():
        out[name] = (out[name] * factor).astype(out[name].dtype)
    return out
```

```python
from contextlib import ExitStack

import numpy as np

import concourse.bass as bass
from concourse import mybir

BATCH, FIELDS, DIM, CROSS, CONTEXT = 512, 39, 16, 128, 16
HIDDEN1, HIDDEN2 = 512, 256
P = 128
GROUPS = P // FIELDS
GF = GROUPS * FIELDS
PARTS = 3
SPT = P // DIM
SPS = SPT * GROUPS
TILES = BATCH // SPT
STEPS = -(-TILES // GROUPS)
LAST_TILES = TILES - (STEPS - 1) * GROUPS
SHIFTS = (FIELDS + 1) // 2
PAIR_CHUNKS = -(-SHIFTS // GROUPS)
FCOLS = FIELDS + 1
YF = 4
Y_CHUNKS = -(-FIELDS // YF)
Y_BANKS = 4
W1_PIECES = 3

INIT_V, INIT_G, MULT_V, ADD_V, ADD_G = range(5)
KIND = [INIT_V, INIT_G, MULT_V, ADD_V, ADD_G, MULT_V, ADD_V, ADD_G, MULT_V, ADD_V]
SLOT = {c: i for i, c in enumerate(c for c in range(Y_CHUNKS) if KIND[c] in (ADD_V, ADD_G))}


def chunk_fields(c):
    return min(YF, FIELDS - c * YF)


PRODUCTS = sum(k != MULT_V for k in KIND)
PRODUCTS_TO = [sum(k != MULT_V for k in KIND[:c + 1]) for c in range(Y_CHUNKS)]
V_OPS_TO = [sum(chunk_fields(i) if KIND[i] == MULT_V else KIND[i] == ADD_V for i in range(c + 1))
            for c in range(Y_CHUNKS)]
V_OPS = V_OPS_TO[-1] + 2
G_OPS_TO = [sum(k == ADD_G for k in KIND[:c + 1]) for c in range(Y_CHUNKS)]
G_OPS = G_OPS_TO[-1] + 1

AT_PARTS, AT_REP_AND_ROWS = 2, 5
AT_SHIFT = [8, 10, 13, 15, 18, 20, 23]
AT_SUM = [11, 13, 16, 18, 21, 23, 26]
SCALAR_LAG, VECTOR_LAG = 0, 2
AT_R0 = 29
AT_S = 6


def program(nc, ids, offsets, table, selectors, mask, w0_upper, w0_lower, w1, w2, dense, wt1,
            wt1_context, bt1, wt2, bt2, wt3, out):
    f32, f32r, bf16, i32 = mybir.dt.float32, mybir.dt.float32r, mybir.dt.bfloat16, mybir.dt.int32
    ALU, ACT, AX = mybir.AluOpType, mybir.ActivationFunctionType, mybir.AxisListType
    ctx = ExitStack()
    with ctx:
        def sb(name, shape, dtype):
            return ctx.enter_context(nc.sbuf_tensor(name, shape, dtype))

        def ps(name):
            return ctx.enter_context(nc.psum_tensor(name, [P, 512], f32))

        def sem(name):
            return ctx.enter_context(nc.semaphore(name))

        ids_sb = sb("ids_sb", [GF, STEPS * SPT], i32)
        rows_sb = sb("rows_sb", [GF, STEPS * SPT], i32)
        offsets_sb = sb("offsets_sb", [GF, 1], i32)
        sel = sb("sel", [GF, selectors.shape[1]], bf16)
        mask_sb = sb("mask_sb", [P, SPT], f32)
        w0 = sb("w0", [GF, PAIR_CHUNKS * CROSS], f32)
        w1_hi = sb("w1_hi", [P, FIELDS * CROSS], f32r)
        w1_lo = sb("w1_lo", [P, FIELDS * CROSS], f32r)
        w2_sb = sb("w2_sb", [P, FIELDS, CROSS], f32)
        wt1_sb = sb("wt1_sb", [P, 3, HIDDEN1], f32)
        wt1_context_sb = sb("wt1_context_sb", [CONTEXT, HIDDEN1], f32)
        wt2_sb = sb("wt2_sb", [P, HIDDEN1 // P, HIDDEN2], f32)
        wt3_sb = sb("wt3_sb", [P, HIDDEN2 // P], f32)
        bt1_sb = sb("bt1_sb", [P, HIDDEN1 // P], f32)
        bt2_sb = sb("bt2_sb", [P, HIDDEN2 // P], f32)
        dense_sb = sb("dense_sb", [CONTEXT, BATCH], f32)
        rows_now = sb("rows_now", [GF, 2, SPT], i32)
        gathered = sb("gathered", [GF, 2, P], f32)
        rest = sb("rest", [GF, 2, P], f32)
        parts = sb("parts", [GF, PARTS, P], bf16)
        x0_parts = sb("x0_parts", [GF, GROUPS * P], bf16)
        x0_rep = sb("x0_rep", [GF, GROUPS * P], f32)
        pairs = sb("pairs", [GF, 2, GROUPS * P], f32)
        x0_rows = sb("x0_rows", [P, 2, GROUPS, FCOLS], f32)
        x0_diag = sb("x0_diag", [P, 2, GROUPS, SPT * FCOLS], f32)
        x1_hi = sb("x1_hi", [P, 2, GROUPS * P], f32r)
        x1_lo = sb("x1_lo", [P, 2, GROUPS * P], f32r)
        prod = sb("prod", [P, len(SLOT), YF * CROSS], f32)
        acc_v = sb("acc_v", [P, 2, YF * CROSS], f32)
        acc_g = sb("acc_g", [P, 2, YF * CROSS], f32)
        x2 = sb("x2", [P, 2, CROSS], f32)
        r0 = sb("r0", [P, BATCH], f32)
        r2 = sb("r2", [P, BATCH], f32)
        S = sb("S", [P, FCOLS, BATCH], f32)
        S_flat = S[:, :, :].rearrange("p f b -> p (f b)")
        w1_raw = S_flat[:, 0:FIELDS * CROSS]
        w0_raw = [S_flat[0:GF, 10 * BATCH + i * PAIR_CHUNKS * CROSS:
                         10 * BATCH + (i + 1) * PAIR_CHUNKS * CROSS] for i in range(2)]
        h1 = prod[:, 0:HIDDEN1 // P, :]
        h2 = acc_v
        y_sb = r2[0:1, :]

        y_ps = [ps(f"y_ps{i}") for i in range(Y_BANKS)]
        pick_ps = [ps("pick_ps0"), ps("pick_ps1")]
        x1_ps = ps("x1_ps")
        s_ps = ps("s_ps")

        h_ps, r2_ps = y_ps, pick_ps[1]

        ids_loaded, sel_loaded, w0_loaded = sem("ids_loaded"), sem("sel_loaded"), sem("w0_loaded")
        w1_loaded = [sem(f"w1_loaded{i}") for i in range(W1_PIECES)]
        mask_loaded, w2_loaded, mlp_loaded = sem("mask_loaded"), sem("w2_loaded"), sem("mlp_loaded")
        rows_known = sem("rows_known")
        rows_taken = sem("rows_taken")
        gather_done = [sem("gather_done0"), sem("gather_done1")]
        waits_over = sem("waits_over")
        split_op = sem("split_op")
        parts_ready = sem("parts_ready")
        diag_ready = sem("diag_ready")
        g_op = sem("g_op")
        acc_g_ready = sem("acc_g_ready")
        ones_set = sem("ones_set")
        w0_ready = sem("w0_ready")
        w1_hi_ready = sem("w1_hi_ready")
        w1_lo_ready = sem("w1_lo_ready")
        picked_parts, picked_rep = sem("picked_parts"), sem("picked_rep")
        picked_rows, picked_shift = sem("picked_rows"), sem("picked_shift")
        parts_copied, rows_copied = sem("parts_copied"), sem("rows_copied")
        rep_copied = sem("rep_copied")
        pairs_ready = sem("pairs_ready")
        pairs_used = sem("pairs_used")
        x1_hi_ready = sem("x1_hi_ready")
        x1_lo_ready = sem("x1_lo_ready")
        r0_ready = sem("r0_ready")
        y_for_scalar, y_for_vector = sem("y_for_scalar"), sem("y_for_vector")
        prod_ready = sem("prod_ready")
        v_op = sem("v_op")
        x2_ready = sem("x2_ready")
        s_made = sem("s_made")
        s_copied = sem("s_copied")
        r2_made, r2_ready = sem("r2_made"), sem("r2_ready")
        h1_made, h2_made, y_made = sem("h1_made"), sem("h2_made"), sem("y_made")
        h1_ready = [sem("h1_by_scalar"), sem("h1_by_vector")]
        h2_ready = [sem("h2_by_scalar"), sem("h2_by_vector")]
        y_ready, out_written = sem("y_ready"), sem("out_written")

        def sel_part(part, j):
            at = (part * GROUPS + j) * GF
            return sel[:, at:at + GF]

        sel_rep_at = PARTS * GROUPS * GF

        def pair_rows(c):
            return FIELDS * min(GROUPS, SHIFTS - c * GROUPS)

        def sel_shift(c):
            at = sel_rep_at + (1 + c) * GF
            return sel[:, at:at + pair_rows(c)]

        def wait(engine, semaphore, value):
            if not isinstance(value, int) or value > 0:
                engine.wait_ge(semaphore, value)

        def y_bank(c, tp):
            return y_ps[(tp * Y_CHUNKS + c) % Y_BANKS]

        def wait_chunk_used(engine, c, n):
            if KIND[c] == MULT_V:
                wait(engine, v_op, n * V_OPS + V_OPS_TO[c])
            else:
                wait(engine, prod_ready, n * PRODUCTS + PRODUCTS_TO[c])

        def tiles_of(s):
            return LAST_TILES if isinstance(s, int) and s == STEPS - 1 else GROUPS

        def has(s, ahead):
            return not isinstance(s, int) or s + ahead < STEPS

        def run_steps(engine, step):
            step(0, 0)
            step(1, 1)
            with engine.Fori(1, STEPS // 2 - 1) as k:
                step(k * 2, 0)
                step(k * 2 + 1, 1)
            step(STEPS - 2, 0)
            step(STEPS - 1, 1)

        block = ctx.enter_context(nc.Block())

        @block.sync
        def _(sp):
            sp.dma_start(ids_sb[:, :], ids).then_inc(ids_loaded, 16)
            sp.dma_start(offsets_sb[:, :], offsets).then_inc(ids_loaded, 16)
            sp.dma_start(sel[:, :], selectors).then_inc(sel_loaded, 16)
            sp.dma_start(w0_raw[0], w0_upper).then_inc(w0_loaded, 16)
            sp.dma_start(w0_raw[1], w0_lower).then_inc(w0_loaded, 16)
            sp.dma_start(mask_sb[:, :], mask).then_inc(mask_loaded, 16)
            cols = FIELDS * CROSS // W1_PIECES
            for i in range(W1_PIECES):
                sp.dma_start(w1_raw[:, i * cols:(i + 1) * cols],
                             w1[:, i * cols:(i + 1) * cols]).then_inc(w1_loaded[i], 16)
            sp.dma_start(w2_sb[:, :, :], w2).then_inc(w2_loaded, 16)
            for dst, src in ((wt1_sb[:, :, :], wt1), (wt1_context_sb[:, :], wt1_context),
                             (wt2_sb[:, :, :], wt2), (wt3_sb[:, :], wt3), (bt1_sb[:, :], bt1),
                             (bt2_sb[:, :], bt2), (dense_sb[:, :], dense)):
                sp.dma_start(dst, src).then_inc(mlp_loaded, 16)
            sp.wait_ge(y_ready, 1)
            sp.dma_start(out, y_sb[:, :]).then_inc(out_written, 16)
            sp.wait_ge(out_written, 16)

        @block.gpsimd
        def _(gp):
            def take_rows(s, par, pair):
                wait(gp, gather_done[par], pair * SPT * 16)
                gp.sem_inc(waits_over, 1)
                nc.gpsimd.tensor_copy(rows_now[:, par, :],
                                      rows_sb[:, bass.ds(s * SPT, SPT)]).then_inc(rows_taken, 1)

            def gather(s, par, which):
                gp.wait_ge(rows_taken, s + 1)
                wait(gp, parts_ready, s - 1)
                gp.sem_inc(waits_over, 1)
                for r in which:
                    nc.gpsimd.indirect_dma_start(
                        out=gathered[:, par, r * DIM:(r + 1) * DIM], out_offset=None, in_=table,
                        in_offset=bass.IndirectOffsetOnAxis(ap=rows_now[:, par, r:r + 1], axis=0),
                    ).then_inc(gather_done[par], 16)

            def split(s, par, pair):
                gp.wait_ge(gather_done[par], (pair + 1) * SPT * 16)
                wait(gp, picked_parts, s)
                gp.sem_inc(waits_over, 1)
                nc.gpsimd.tensor_copy(parts[:, 0, :], gathered[:, par, :]).then_inc(split_op, 1)
                gp.wait_ge(split_op, s * 4 + 1)
                nc.gpsimd.tensor_tensor(rest[:, 0, :], gathered[:, par, :], parts[:, 0, :],
                                        ALU.subtract).then_inc(split_op, 1)
                gp.wait_ge(split_op, s * 4 + 2)
                gp.sem_inc(waits_over, 1)
                nc.gpsimd.tensor_copy(parts[:, 1, :], rest[:, 0, :]).then_inc(split_op, 1)
                gp.wait_ge(split_op, s * 4 + 3)
                nc.gpsimd.tensor_tensor(rest[:, 1, :], rest[:, 0, :], parts[:, 1, :],
                                        ALU.subtract).then_inc(split_op, 1)
                gp.wait_ge(split_op, s * 4 + 4)
                gp.sem_inc(waits_over, 1)
                nc.gpsimd.tensor_copy(parts[:, 2, :], rest[:, 1, :]).then_inc(parts_ready, 1)

            def diag(s, par, t):
                gp.wait_ge(rows_copied, s + 1)
                wait(gp, s_made, (s - 1) * GROUPS)
                nc.gpsimd.tensor_tensor(
                    x0_diag[:, par, t, :].rearrange("p (b f) -> p b f", f=FCOLS),
                    x0_rows[:, par, t, :].unsqueeze(1).to_broadcast([P, SPT, FCOLS]),
                    mask_sb[:, :].unsqueeze(2).to_broadcast([P, SPT, FCOLS]),
                    ALU.mult).then_inc(diag_ready, 1)

            def add(s, par, t, c):
                n, tp = s * GROUPS + t, (par * GROUPS + t) % 2
                width = chunk_fields(c) * CROSS
                gp.wait_ge(prod_ready, n * PRODUCTS + PRODUCTS_TO[c])
                wait(gp, g_op, n * G_OPS + G_OPS_TO[c] - 1)
                nc.gpsimd.tensor_tensor(acc_g[:, tp, 0:width], acc_g[:, tp, 0:width],
                                        prod[:, SLOT[c], 0:width], ALU.add).then_inc(g_op, 1)

            def fold(s, par, t):
                n, tp = s * GROUPS + t, (par * GROUPS + t) % 2
                gp.wait_ge(g_op, n * G_OPS + G_OPS - 1)
                nc.gpsimd.tensor_tensor(acc_g[:, tp, 0:2 * CROSS], acc_g[:, tp, 0:2 * CROSS],
                                        acc_g[:, tp, 2 * CROSS:4 * CROSS], ALU.add).then_inc(g_op, 1)
                gp.wait_ge(g_op, n * G_OPS + G_OPS)
                nc.gpsimd.tensor_tensor(acc_g[:, tp, 0:CROSS], acc_g[:, tp, 0:CROSS],
                                        acc_g[:, tp, CROSS:2 * CROSS], ALU.add).then_inc(acc_g_ready, 1)

            def step(s, par, pair):
                ahead = has(s, 2)
                if ahead:
                    take_rows(s + 2, par, pair + 1)
                for t in range(tiles_of(s)):
                    for i, c in enumerate(c for c in range(Y_CHUNKS) if KIND[c] == ADD_G):
                        if ahead and t < 2:
                            first = t * SPT // 2
                            gather(s + 2, par, range(first, first + 3) if i == 0
                                   else range(first + 3, first + SPT // 2) if i == 1 else ())
                        add(s, par, t, c)
                        if ahead and t == 2 and i == 0:
                            split(s + 2, par, pair + 1)
                    fold(s, par, t)
                    if has(s, 1) and t < tiles_of(s + 1):
                        diag(s + 1, 1 - par, t)

            gp.wait_ge(ids_loaded, 32)
            nc.gpsimd.tensor_tensor(rows_sb[:, :], ids_sb[:, :],
                                    offsets_sb[:, :].to_broadcast([GF, STEPS * SPT]),
                                    ALU.add).then_inc(rows_known, 1)
            gp.wait_ge(rows_known, 1)
            take_rows(0, 0, 0)
            gather(0, 0, range(SPT))
            split(0, 0, 0)
            take_rows(1, 1, 0)
            gather(1, 1, range(SPT))
            gp.wait_ge(mask_loaded, 16)
            gp.wait_ge(ones_set, 1)
            for t in range(GROUPS):
                diag(0, 0, t)
            split(1, 1, 0)
            step(0, 0, 0)
            step(1, 1, 0)
            with gp.Fori(1, STEPS // 2 - 1) as k:
                step(k * 2, 0, k)
                step(k * 2 + 1, 1, k)
            step(STEPS - 2, 0, STEPS // 2 - 1)
            step(STEPS - 1, 1, STEPS // 2 - 1)

        @block.scalar
        def _(act):
            def copy_parts(s, par):
                width = tiles_of(s) * P
                act.wait_ge(picked_parts, s + 1)
                wait(act, picked_shift, s * PAIR_CHUNKS)
                nc.scalar.activation(x0_parts[:, 0:width], pick_ps[1][0:GF, 0:width],
                                     ACT.Copy).then_inc(parts_copied, 1)

            def copy_rows(s, par):
                tiles = tiles_of(s)
                act.wait_ge(picked_rows, s + 1)
                wait(act, x2_ready, (s - 1) * GROUPS)
                wait(act, diag_ready, (s - 1) * GROUPS)
                nc.scalar.activation(
                    x0_rows[:, par, 0:tiles, 0:FIELDS],
                    pick_ps[1][:, 0:tiles * FIELDS].rearrange("p (t f) -> p t f", f=FIELDS),
                    ACT.Copy).then_inc(rows_copied, 1)

            def round_x1(s, par):
                width = tiles_of(s) * P
                act.wait_ge(pairs_used, (s + 1) * PAIR_CHUNKS)
                nc.scalar.activation(x1_hi[:, par, 0:width], x1_ps[:, 0:width],
                                     ACT.Copy).then_inc(x1_hi_ready, 1)

            def copy_s(s, t):
                n = s * GROUPS + t
                act.wait_ge(s_made, n + 1)
                nc.scalar.activation(
                    S[:, :, bass.ds(s * SPS + t * SPT, SPT)],
                    s_ps[:, 0:SPT * FCOLS].rearrange("p (b f) -> p f b", f=FCOLS),
                    ACT.Copy).then_inc(s_copied, 1)

            def multiply(s, par, t, c):
                n, tp = s * GROUPS + t, (par * GROUPS + t) % 2
                act.wait_ge(y_for_scalar, n * PRODUCTS + PRODUCTS_TO[c])
                if KIND[c] in (INIT_V, INIT_G):
                    wait(act, x2_ready, n - 1)
                    into = (acc_v if KIND[c] == INIT_V else acc_g)[:, tp, :]
                else:
                    if KIND[c] == ADD_V:
                        wait(act, v_op, (n - 1) * V_OPS + V_OPS_TO[c])
                    else:
                        wait(act, g_op, (n - 1) * G_OPS + G_OPS_TO[c])
                    into = prod[:, SLOT[c], :]
                for i in range(chunk_fields(c)):
                    f = c * YF + i
                    last = nc.scalar.activation(
                        into[:, i * CROSS:(i + 1) * CROSS],
                        y_bank(c, tp)[:, i * CROSS:(i + 1) * CROSS], ACT.Copy,
                        scale=x0_rows[:, par, t, f:f + 1])
                last.then_inc(prod_ready, 1)

            def step(s, par):
                act.wait_ge(rows_copied, s + 1)
                for t in range(tiles_of(s)):
                    for c in range(Y_CHUNKS):
                        at = t * Y_CHUNKS + c
                        if KIND[c] != MULT_V:
                            multiply(s, par, t, c)
                        if has(s, 1):
                            if at - SCALAR_LAG == AT_PARTS:
                                copy_parts(s + 1, 1 - par)
                            if at - SCALAR_LAG == AT_REP_AND_ROWS:
                                copy_rows(s + 1, 1 - par)
                            if at - SCALAR_LAG == AT_SUM[-1]:
                                round_x1(s + 1, 1 - par)
                        if c - SCALAR_LAG == AT_S:
                            if t > 0:
                                copy_s(s, t - 1)
                            elif not isinstance(s, int) or s > 0:
                                copy_s(s - 1, GROUPS - 1)

            copy_parts(0, 0)
            act.wait_ge(ones_set, 1)
            copy_rows(0, 0)
            cols = FIELDS * CROSS // W1_PIECES
            for i in range(W1_PIECES):
                act.wait_ge(w1_loaded[i], 16)
                nc.scalar.activation(w1_hi[:, i * cols:(i + 1) * cols],
                                     w1_raw[:, i * cols:(i + 1) * cols],
                                     ACT.Copy).then_inc(w1_hi_ready, 1)
            round_x1(0, 0)
            run_steps(act, step)
            copy_s(STEPS - 1, LAST_TILES - 1)

            act.wait_ge(mlp_loaded, 7 * 16)
            for m in range(0, HIDDEN1 // P, 2):
                act.wait_ge(h1_made, m + 1)
                nc.scalar.activation(h1[:, m, :], h_ps[m][:, :], ACT.Relu,
                                     bias=bt1_sb[:, m:m + 1]).then_inc(h1_ready[0], 1)
            act.wait_ge(h2_made, 1)
            nc.scalar.activation(h2[:, 0, :], pick_ps[0][:, :], ACT.Relu,
                                 bias=bt2_sb[:, 0:1]).then_inc(h2_ready[0], 1)

        @block.vector
        def _(dve):
            def copy_rep(s, par):
                width = tiles_of(s) * P
                dve.wait_ge(picked_rep, s + 1)
                nc.vector.tensor_copy(x0_rep[:, 0:width], pick_ps[0][0:GF, 0:width]).then_inc(rep_copied, 1)

            def multiply_pairs(s, par, c):
                width, rows, i = tiles_of(s) * P, pair_rows(c), s * PAIR_CHUNKS + c
                buf = (par * PAIR_CHUNKS + c) % 2
                dve.wait_ge(rep_copied, s + 1)
                dve.wait_ge(picked_shift, i + 1)
                wait(dve, pairs_used, i - 1)
                nc.vector.tensor_tensor(pairs[0:rows, buf, 0:width], x0_rep[0:rows, 0:width],
                                        pick_ps[c % 2][0:rows, 0:width], ALU.mult).then_inc(pairs_ready, 1)

            def rest_of_x1(s, par):
                width = tiles_of(s) * P
                dve.wait_ge(x1_hi_ready, s + 1)
                nc.vector.tensor_tensor(x1_lo[:, par, 0:width], x1_ps[:, 0:width],
                                        x1_hi[:, par, 0:width], ALU.subtract).then_inc(x1_lo_ready, 1)

            def sum_x1(s, par):
                tiles = tiles_of(s)
                nc.vector.tensor_reduce(
                    r0[:, bass.ds(s * SPS, tiles * SPT)],
                    x1_ps[:, 0:tiles * P].rearrange("p (b d) -> p b d", d=DIM),
                    axis=AX.X, op=ALU.add).then_inc(r0_ready, 1)

            def accumulate(s, par, t, c):
                n, tp = s * GROUPS + t, (par * GROUPS + t) % 2
                before = n * V_OPS + (V_OPS_TO[c - 1] if c else 0)
                if KIND[c] == MULT_V:
                    dve.wait_ge(y_for_vector, n * (Y_CHUNKS - PRODUCTS) + c + 1 - PRODUCTS_TO[c])
                    for i in range(chunk_fields(c)):
                        f, lane = c * YF + i, acc_v[:, tp, i * CROSS:(i + 1) * CROSS]
                        if i == 0:
                            dve.wait_ge(prod_ready, n * PRODUCTS + PRODUCTS_TO[0])
                            wait(dve, v_op, before)
                        nc.vector.scalar_tensor_tensor(
                            lane, y_bank(c, tp)[:, i * CROSS:(i + 1) * CROSS],
                            x0_rows[:, par, t, f:f + 1], lane, ALU.mult, ALU.add).then_inc(v_op, 1)
                else:
                    width = chunk_fields(c) * CROSS
                    dve.wait_ge(prod_ready, n * PRODUCTS + PRODUCTS_TO[c])
                    wait(dve, v_op, before)
                    nc.vector.tensor_tensor(acc_v[:, tp, 0:width], acc_v[:, tp, 0:width],
                                            prod[:, SLOT[c], 0:width], ALU.add).then_inc(v_op, 1)

            def fold(s, par, t):
                n, tp = s * GROUPS + t, (par * GROUPS + t) % 2
                dve.wait_ge(v_op, n * V_OPS + V_OPS - 2)
                nc.vector.tensor_tensor(acc_v[:, tp, 0:2 * CROSS], acc_v[:, tp, 0:2 * CROSS],
                                        acc_v[:, tp, 2 * CROSS:4 * CROSS], ALU.add).then_inc(v_op, 1)
                dve.wait_ge(v_op, n * V_OPS + V_OPS - 1)
                nc.vector.tensor_tensor(acc_v[:, tp, 0:CROSS], acc_v[:, tp, 0:CROSS],
                                        acc_v[:, tp, CROSS:2 * CROSS], ALU.add).then_inc(v_op, 1)
                dve.wait_ge(v_op, n * V_OPS + V_OPS)
                dve.wait_ge(acc_g_ready, n + 1)
                wait(dve, s_made, n - 1)
                nc.vector.tensor_tensor(x2[:, tp, :], acc_v[:, tp, 0:CROSS], acc_g[:, tp, 0:CROSS],
                                        ALU.add).then_inc(x2_ready, 1)

            def step(s, par):
                dve.wait_ge(rows_copied, s + 1)
                for t in range(tiles_of(s)):
                    for c in range(Y_CHUNKS):
                        at = t * Y_CHUNKS + c
                        if KIND[c] in (MULT_V, ADD_V):
                            accumulate(s, par, t, c)
                        if has(s, 1):
                            if at + VECTOR_LAG == AT_REP_AND_ROWS:
                                copy_rep(s + 1, 1 - par)
                            if at + VECTOR_LAG in AT_SHIFT:
                                multiply_pairs(s + 1, 1 - par, AT_SHIFT.index(at + VECTOR_LAG))
                            if at + VECTOR_LAG == AT_SUM[-1] + 1:
                                rest_of_x1(s + 1, 1 - par)
                            if at == AT_R0:
                                sum_x1(s + 1, 1 - par)
                    fold(s, par, t)

            nc.vector.memset(x0_rows[:, :, :, FIELDS:FCOLS], 1.0).then_inc(ones_set, 1)
            dve.wait_ge(w0_loaded, 32)
            nc.vector.tensor_tensor(w0[:, :], w0_raw[0], w0_raw[1], ALU.add).then_inc(w0_ready, 1)
            copy_rep(0, 0)
            multiply_pairs(0, 0, 0)
            cols = FIELDS * CROSS // W1_PIECES
            for c in range(1, PAIR_CHUNKS):
                multiply_pairs(0, 0, c)
                if c % 2 == 0:
                    i = c // 2 - 1
                    dve.wait_ge(w1_hi_ready, i + 1)
                    nc.vector.tensor_tensor(w1_lo[:, i * cols:(i + 1) * cols],
                                            w1_raw[:, i * cols:(i + 1) * cols],
                                            w1_hi[:, i * cols:(i + 1) * cols],
                                            ALU.subtract).then_inc(w1_lo_ready, 1)
            rest_of_x1(0, 0)
            sum_x1(0, 0)
            run_steps(dve, step)

            dve.wait_ge(r2_made, 1)
            nc.vector.tensor_copy(r2[:, :], r2_ps[:, :]).then_inc(r2_ready, 1)
            dve.wait_ge(mlp_loaded, 7 * 16)
            for m in range(1, HIDDEN1 // P, 2):
                dve.wait_ge(h1_made, m + 1)
                nc.vector.tensor_scalar(h1[:, m, :], h_ps[m][:, :], bt1_sb[:, m:m + 1], 0.0,
                                        ALU.add, ALU.max).then_inc(h1_ready[1], 1)
            dve.wait_ge(h2_made, 2)
            nc.vector.tensor_scalar(h2[:, 1, :], x1_ps[:, :], bt2_sb[:, 1:2], 0.0,
                                    ALU.add, ALU.max).then_inc(h2_ready[1], 1)
            dve.wait_ge(y_made, 1)
            nc.vector.tensor_copy(y_sb[:, :], s_ps[0:1, :]).then_inc(y_ready, 1)

        @block.tensor
        def _(pe):
            mm = nc.tensor.matmul

            def pick_parts(s, par):
                pe.wait_ge(parts_ready, s + 1)
                wait(pe, pairs_ready, s * PAIR_CHUNKS)
                for j in range(tiles_of(s)):
                    for part in range(PARTS):
                        last = mm(pick_ps[1][0:GF, j * P:(j + 1) * P], sel_part(part, j), parts[:, part, :],
                                  start=part == 0, stop=part == PARTS - 1)
                last.then_inc(picked_parts, 1)

            def pick_rep(s, par):
                width = tiles_of(s) * P
                pe.wait_ge(parts_copied, s + 1)
                mm(pick_ps[0][0:GF, 0:width], sel[:, sel_rep_at:sel_rep_at + GF], x0_parts[:, 0:width],
                   start=True, stop=True).then_inc(picked_rep, 1)

            def pick_rows(s, par):
                for j in range(tiles_of(s)):
                    last = mm(pick_ps[1][:, j * FIELDS:(j + 1) * FIELDS], x0_parts[:, j * P:(j + 1) * P],
                              sel[:, sel_rep_at:sel_rep_at + FIELDS], start=True, stop=True)
                last.then_inc(picked_rows, 1)

            def pick_shift(s, par, c):
                width = tiles_of(s) * P
                if c == 0:
                    pe.wait_ge(rep_copied, s + 1)
                elif c == 1:
                    pe.wait_ge(rows_copied, s + 1)
                else:
                    pe.wait_ge(pairs_ready, s * PAIR_CHUNKS + c - 1)
                mm(pick_ps[c % 2][0:pair_rows(c), 0:width], sel_shift(c), x0_parts[:, 0:width],
                   start=True, stop=True).then_inc(picked_shift, 1)

            def sum_pairs(s, par, c):
                width, rows, i = tiles_of(s) * P, pair_rows(c), s * PAIR_CHUNKS + c
                pe.wait_ge(pairs_ready, i + 1)
                if c == 0:
                    wait(pe, r0_ready, s)
                mm(x1_ps[:, 0:width], w0[0:rows, c * CROSS:(c + 1) * CROSS],
                   pairs[0:rows, (par * PAIR_CHUNKS + c) % 2, 0:width],
                   start=c == 0, stop=c == PAIR_CHUNKS - 1).then_inc(pairs_used, 1)

            def y_chunk(s, par, t, c):
                n, width = s * GROUPS + t, chunk_fields(c) * CROSS
                tp = (par * GROUPS + t) % 2
                if c >= Y_BANKS:
                    wait_chunk_used(pe, c - Y_BANKS, n)
                elif not isinstance(n, int) or n > 0:
                    wait_chunk_used(pe, c + Y_CHUNKS - Y_BANKS, n - 1)
                y = y_bank(c, tp)[:, 0:width]
                w = slice(c * YF * CROSS, c * YF * CROSS + width)
                hi, lo = x1_hi[:, par, t * P:(t + 1) * P], x1_lo[:, par, t * P:(t + 1) * P]
                mm(y, hi, w1_hi[:, w], start=True, stop=False)
                mm(y, hi, w1_lo[:, w], start=False, stop=False)
                mm(y, lo, w1_hi[:, w], start=False, stop=True).then_inc(
                    y_for_vector if KIND[c] == MULT_V else y_for_scalar, 1)

            def make_s(s, par, t):
                n, tp = s * GROUPS + t, (par * GROUPS + t) % 2
                pe.wait_ge(x2_ready, n + 1)
                pe.wait_ge(diag_ready, n + 1)
                wait(pe, s_copied, n)
                mm(s_ps[:, 0:SPT * FCOLS], x2[:, tp, :], x0_diag[:, par, t, :],
                   start=True, stop=True).then_inc(s_made, 1)

            def step(s, par):
                pe.wait_ge(x1_hi_ready, s + 1)
                pe.wait_ge(x1_lo_ready, s + 1)
                if isinstance(s, int) and s == 0:
                    pe.wait_ge(w1_lo_ready, W1_PIECES)
                for t in range(tiles_of(s)):
                    for c in range(Y_CHUNKS):
                        at = t * Y_CHUNKS + c
                        y_chunk(s, par, t, c)
                        if has(s, 1):
                            if at == AT_PARTS:
                                pick_parts(s + 1, 1 - par)
                            if at == AT_REP_AND_ROWS:
                                pick_rep(s + 1, 1 - par)
                                pick_rows(s + 1, 1 - par)
                            if at in AT_SUM:
                                sum_pairs(s + 1, 1 - par, AT_SUM.index(at))
                            if at in AT_SHIFT:
                                pick_shift(s + 1, 1 - par, AT_SHIFT.index(at))
                        if c == AT_S:
                            if t > 0:
                                make_s(s, par, t - 1)
                            elif not isinstance(s, int) or s > 0:
                                make_s(s - 1, 1 - par, GROUPS - 1)

            pe.wait_ge(sel_loaded, 16)
            pick_parts(0, 0)
            pick_rep(0, 0)
            pick_rows(0, 0)
            pick_shift(0, 0, 0)
            pe.wait_ge(w0_ready, 1)
            for c in range(PAIR_CHUNKS):
                if c < PAIR_CHUNKS - 1:
                    pick_shift(0, 0, c + 1)
                sum_pairs(0, 0, c)
            run_steps(pe, step)
            make_s(STEPS - 1, 1, LAST_TILES - 1)

            last_tile = TILES - 1
            pe.wait_ge(prod_ready, (last_tile + 1) * PRODUCTS)
            pe.wait_ge(v_op, (last_tile + 1) * V_OPS)
            pe.wait_ge(mlp_loaded, 7 * 16)
            pe.wait_ge(r0_ready, STEPS)
            pe.wait_ge(s_copied, TILES)
            for m in range(HIDDEN1 // P):
                units = slice(m * P, (m + 1) * P)
                mm(h_ps[m][:, :], wt1_sb[:, 0, units], r0[:, :], start=True, stop=False)
                mm(h_ps[m][:, :], wt1_sb[:, 1, units], S[:, FIELDS, :], start=False, stop=False)
                mm(h_ps[m][:, :], wt1_context_sb[:, units], dense_sb[:, :], start=False, stop=False)
            pe.wait_ge(w2_loaded, 16)
            for f in range(FIELDS):
                last = mm(r2_ps[:, :], w2_sb[:, f, :], S[:, f, :], start=f == 0, stop=f == FIELDS - 1)
            last.then_inc(r2_made, 1)
            pe.wait_ge(r2_ready, 1)
            for m in range(HIDDEN1 // P):
                mm(h_ps[m][:, :], wt1_sb[:, 2, m * P:(m + 1) * P], r2[:, :],
                   start=False, stop=True).then_inc(h1_made, 1)
            for k in range(HIDDEN1 // P):
                pe.wait_ge(h1_ready[k % 2], k // 2 + 1)
                for m in range(HIDDEN2 // P):
                    last = mm((pick_ps[0], x1_ps)[m][:, :], wt2_sb[:, k, m * P:(m + 1) * P], h1[:, k, :],
                              start=k == 0, stop=k == HIDDEN1 // P - 1)
                    if k == HIDDEN1 // P - 1:
                        last.then_inc(h2_made, 1)
            for m in range(HIDDEN2 // P):
                pe.wait_ge(h2_ready[m], 1)
                last = mm(s_ps[0:1, :], wt3_sb[:, m:m + 1], h2[:, m, :],
                          start=m == 0, stop=m == HIDDEN2 // P - 1)
            last.then_inc(y_made, 1)


def selector_constants():
    f = np.arange(FIELDS)
    blocks = []
    for part in range(PARTS):
        for j in range(GROUPS):
            m = np.zeros((GF, GF), np.float32)
            m[j * FIELDS + f, part * FIELDS + f] = 1
            blocks.append(m)
    m = np.zeros((GF, GF), np.float32)
    for part in range(PARTS):
        for j in range(GROUPS):
            m[part * FIELDS + f, j * FIELDS + f] = 1
    blocks.append(m)
    for c in range(PAIR_CHUNKS):
        m = np.zeros((GF, GF), np.float32)
        for part in range(PARTS):
            for j in range(GROUPS):
                m[part * FIELDS + (f + c * GROUPS + j) % FIELDS, j * FIELDS + f] = 1
        blocks.append(m)
    return np.concatenate(blocks, axis=1)


def pair_layout(w0):
    w0 = w0.reshape(FIELDS, FIELDS, CROSS)
    upper = np.zeros((GF, PAIR_CHUNKS, CROSS), np.float32)
    lower = np.zeros((GF, PAIR_CHUNKS, CROSS), np.float32)
    f = np.arange(FIELDS)
    for s in range(SHIFTS):
        rows = slice(s % GROUPS * FIELDS, (s % GROUPS + 1) * FIELDS)
        upper[rows, s // GROUPS] = w0[f, (f + s) % FIELDS]
        if s:
            lower[rows, s // GROUPS] = w0[(f + s) % FIELDS, f]
    return upper.reshape(GF, -1), lower.reshape(GF, -1)


def kernel(**inputs):
    import concourse.bacc as bacc
    import ml_dtypes
    from concourse.bass_utils import run_bass_kernel_spmd

    x = {k: np.asarray(v) for k, v in inputs.items()}
    tables = [x[f"tbl_{i}"] for i in range(FIELDS)]
    sizes = [t.shape[0] for t in tables]
    starts = np.concatenate([[0], np.cumsum(sizes)[:-1]]).astype(np.int32)
    ids = np.zeros((STEPS * SPS, FIELDS), np.int32)
    ids[:BATCH] = x["ids"]
    ids = ids.reshape(STEPS, GROUPS, SPT, FIELDS).transpose(1, 3, 0, 2).reshape(GF, STEPS * SPT)
    mask = np.zeros((P, SPT), np.float32)
    mask[np.arange(P), np.arange(P) // DIM] = 1
    upper, lower = pair_layout(x["L0_rec_f0"])

    def by_g(w):
        return w.reshape(FIELDS, CROSS, CROSS).transpose(1, 0, 2)

    wt1 = x["W_top1"]
    arrays = {
        "in_ids": ids,
        "in_offsets": np.tile(starts, GROUPS)[:, None],
        "in_table": np.concatenate(tables, axis=0),
        "in_selectors": selector_constants().astype(ml_dtypes.bfloat16),
        "in_mask": mask,
        "in_w0_upper": upper,
        "in_w0_lower": lower,
        "in_w1": by_g(x["L0_rec_f1"]).reshape(P, FIELDS * CROSS),
        "in_w2": by_g(x["L0_rec_f2"]),
        "in_dense": x["dense_ctx"].T,
        "in_wt1": wt1[:3 * P].reshape(3, P, HIDDEN1).transpose(1, 0, 2),
        "in_wt1_context": wt1[3 * P:],
        "in_bt1": x["b_top1"].reshape(-1, P).T,
        "in_wt2": x["W_top2"].reshape(-1, P, HIDDEN2).transpose(1, 0, 2),
        "in_bt2": x["b_top2"].reshape(-1, P).T,
        "in_wt3": x["W_top3"].reshape(-1, P).T,
    }
    arrays = {k: np.ascontiguousarray(v) for k, v in arrays.items()}
    nc = bacc.Bacc("TRN2", target_bir_lowering=False, num_devices=1)
    args = [nc.dram_tensor(k, v.shape, mybir.dt.from_np(v.dtype), kind="ExternalInput").ap()
            for k, v in arrays.items()]
    out = nc.dram_tensor("out_y", (1, BATCH), mybir.dt.float32, kind="ExternalOutput").ap()
    program(nc, *args, out)
    r = run_bass_kernel_spmd(nc, [arrays], core_ids=[0])
    return r.results[0]["out_y"].reshape(BATCH, 1)
```

```python
from contextlib import ExitStack

import numpy as np

import concourse.bass as bass
from concourse import mybir

BATCH, FIELDS, DIM, CROSS, CONTEXT = 512, 39, 16, 128, 16
HIDDEN1, HIDDEN2 = 512, 256
P = 128
GROUPS = P // FIELDS
GF = GROUPS * FIELDS
SPT = P // DIM
SPS = SPT * GROUPS
TILES = BATCH // SPT
STEPS = -(-TILES // GROUPS)
LAST_TILES = TILES - (STEPS - 1) * GROUPS
SHIFTS = (FIELDS + 1) // 2
PAIR_CHUNKS = -(-SHIFTS // GROUPS)
FCOLS = FIELDS + 1
YF = 4
Y_CHUNKS = -(-FIELDS // YF)
Y_BANKS = 5
W1_PIECES = 3

INIT_V, INIT_G, MULT_V, ADD_V, ADD_G = range(5)
KIND = [INIT_V, INIT_G, MULT_V, ADD_V, ADD_G, MULT_V, ADD_V, ADD_G, MULT_V, ADD_V]
SLOT = {c: i for i, c in enumerate(c for c in range(Y_CHUNKS) if KIND[c] in (ADD_V, ADD_G))}


def chunk_fields(c):
    return min(YF, FIELDS - c * YF)


PRODUCTS = sum(k != MULT_V for k in KIND)
PRODUCTS_TO = [sum(k != MULT_V for k in KIND[:c + 1]) for c in range(Y_CHUNKS)]
V_OPS_TO = [sum(chunk_fields(i) if KIND[i] == MULT_V else KIND[i] == ADD_V for i in range(c + 1))
            for c in range(Y_CHUNKS)]
V_OPS = V_OPS_TO[-1] + 2
G_OPS_TO = [sum(k == ADD_G for k in KIND[:c + 1]) for c in range(Y_CHUNKS)]
G_OPS = G_OPS_TO[-1] + 1

AT_ROWS = 2
AT_MULTIPLY = [3, 6, 9, 12, 15, 18, 21]
AT_SUM = [7, 10, 13, 16, 19, 22, 25]
AT_R0 = 29
GATHERS_AT = [(0, 1, 2), (3,), (4, 5, 6), (7,), (), ()]
AT_S = 6


def program(nc, ids, offsets, table, identity, mask, w0_upper, w0_lower, w1, w2, dense, wt1,
            wt1_context, bt1, wt2, bt2, wt3, out):
    f32, f32r, i32 = mybir.dt.float32, mybir.dt.float32r, mybir.dt.int32
    ALU, ACT, AX = mybir.AluOpType, mybir.ActivationFunctionType, mybir.AxisListType
    ctx = ExitStack()
    with ctx:
        def sb(name, shape, dtype):
            return ctx.enter_context(nc.sbuf_tensor(name, shape, dtype))

        def ps(name):
            return ctx.enter_context(nc.psum_tensor(name, [P, 512], f32))

        def sem(name):
            return ctx.enter_context(nc.semaphore(name))

        ids_sb = sb("ids_sb", [GF, STEPS * SPT], i32)
        rows_sb = sb("rows_sb", [GF, STEPS * SPT], i32)
        offsets_sb = sb("offsets_sb", [GF, 1], i32)
        identity_sb = sb("identity_sb", [GF, GF], f32)
        mask_sb = sb("mask_sb", [P, SPT], f32)
        w0 = sb("w0", [GF, PAIR_CHUNKS * CROSS], f32)
        w1_hi = sb("w1_hi", [P, FIELDS * CROSS], f32r)
        w1_lo = sb("w1_lo", [P, FIELDS * CROSS], f32r)
        w2_sb = sb("w2_sb", [P, FIELDS, CROSS], f32)
        wt1_sb = sb("wt1_sb", [P, 3, HIDDEN1], f32)
        wt1_context_sb = sb("wt1_context_sb", [CONTEXT, HIDDEN1], f32)
        wt2_sb = sb("wt2_sb", [P, HIDDEN1 // P, HIDDEN2], f32)
        wt3_sb = sb("wt3_sb", [P, HIDDEN2 // P], f32)
        bt1_sb = sb("bt1_sb", [P, HIDDEN1 // P], f32)
        bt2_sb = sb("bt2_sb", [P, HIDDEN2 // P], f32)
        dense_sb = sb("dense_sb", [CONTEXT, BATCH], f32)
        rows_now = sb("rows_now", [GF, 2, SPT], i32)
        gathered = sb("gathered", [GF, 2, P], f32)
        x0_rep = sb("x0_rep", [GF, GROUPS * P], f32)
        x0_shifted = sb("x0_shifted", [GF, PAIR_CHUNKS, GROUPS * P], f32)
        pairs = sb("pairs", [GF, 2, GROUPS * P], f32)
        x0_rows = sb("x0_rows", [P, 2, GROUPS, FCOLS], f32)
        x0_diag = sb("x0_diag", [P, 2, SPT * FCOLS], f32)
        x1_hi = sb("x1_hi", [P, 2, GROUPS * P], f32r)
        x1_lo = sb("x1_lo", [P, 2, GROUPS * P], f32r)
        prod = sb("prod", [P, len(SLOT), YF * CROSS], f32)
        acc_v = sb("acc_v", [P, 2, YF * CROSS], f32)
        acc_g = sb("acc_g", [P, 2, YF * CROSS], f32)
        x2 = sb("x2", [P, 2, CROSS], f32)
        r0 = sb("r0", [P, BATCH], f32)
        r2 = sb("r2", [P, BATCH], f32)
        S = sb("S", [P, FCOLS, BATCH], f32)
        S_flat = S[:, :, :].rearrange("p f b -> p (f b)")
        w1_raw = S_flat[:, 0:FIELDS * CROSS]
        w0_raw = [S_flat[0:GF, 10 * BATCH + i * PAIR_CHUNKS * CROSS:
                         10 * BATCH + (i + 1) * PAIR_CHUNKS * CROSS] for i in range(2)]
        h1 = prod[:, 0:HIDDEN1 // P, :]
        h2 = acc_v
        y_sb = r2[0:1, :]

        y_ps = [ps(f"y_ps{i}") for i in range(Y_BANKS)]
        rows_ps = ps("rows_ps")
        x1_ps = ps("x1_ps")
        s_ps = ps("s_ps")

        h_ps, r2_ps = y_ps[1:], y_ps[0]
        scratch = [nc.dram_tensor(f"x0_scratch{i}", [2, FIELDS, GROUPS * P], f32).ap()
                   for i in range(2)]

        ids_loaded, w0_loaded = sem("ids_loaded"), sem("w0_loaded")
        identity_loaded = sem("identity_loaded")
        w1_loaded = [sem(f"w1_loaded{i}") for i in range(W1_PIECES)]
        mask_loaded, w2_loaded, mlp_loaded = sem("mask_loaded"), sem("w2_loaded"), sem("mlp_loaded")
        rows_known = sem("rows_known")
        rows_taken = sem("rows_taken")
        gather_done = [sem("gather_done0"), sem("gather_done1")]
        waits_over = sem("waits_over")
        sp_waits_over = sem("sp_waits_over")
        scratch_written = [sem("scratch_written0"), sem("scratch_written1")]
        x0_loaded = sem("x0_loaded")
        diag_ready = sem("diag_ready")
        g_op = sem("g_op")
        acc_g_ready = sem("acc_g_ready")
        ones_set = sem("ones_set")
        w0_ready = sem("w0_ready")
        w1_hi_ready = sem("w1_hi_ready")
        w1_lo_ready = sem("w1_lo_ready")
        transposed = sem("transposed")
        rows_copied = sem("rows_copied")
        pairs_ready = sem("pairs_ready")
        pairs_used = sem("pairs_used")
        x1_hi_ready = sem("x1_hi_ready")
        x1_lo_ready = sem("x1_lo_ready")
        r0_ready = sem("r0_ready")
        y_for_scalar, y_for_vector = sem("y_for_scalar"), sem("y_for_vector")
        prod_ready = sem("prod_ready")
        v_op = sem("v_op")
        x2_ready = sem("x2_ready")
        s_made = sem("s_made")
        s_copied = sem("s_copied")
        r2_made, r2_ready = sem("r2_made"), sem("r2_ready")
        h1_made, h2_made, y_made = sem("h1_made"), sem("h2_made"), sem("y_made")
        h1_ready = [sem("h1_by_scalar"), sem("h1_by_vector")]
        h2_ready = [sem("h2_by_scalar"), sem("h2_by_vector")]
        y_ready, out_written = sem("y_ready"), sem("out_written")

        def pair_rows(c):
            return FIELDS * min(GROUPS, SHIFTS - c * GROUPS)

        def wait(engine, semaphore, value):
            if not isinstance(value, int) or value > 0:
                engine.wait_ge(semaphore, value)

        def y_bank(c):
            return y_ps[c % Y_BANKS]

        def wait_chunk_used(engine, c, n):
            if KIND[c] == MULT_V:
                wait(engine, v_op, n * V_OPS + V_OPS_TO[c])
            else:
                wait(engine, prod_ready, n * PRODUCTS + PRODUCTS_TO[c])

        def tiles_of(s):
            return LAST_TILES if isinstance(s, int) and s == STEPS - 1 else GROUPS

        def has(s, ahead):
            return not isinstance(s, int) or s + ahead < STEPS

        def run_steps(engine, step):
            step(0, 0, 0)
            step(1, 1, 0)
            with engine.Fori(1, STEPS // 2 - 1) as k:
                step(k * 2, 0, k)
                step(k * 2 + 1, 1, k)
            step(STEPS - 2, 0, STEPS // 2 - 1)
            step(STEPS - 1, 1, STEPS // 2 - 1)

        block = ctx.enter_context(nc.Block())

        @block.sync
        def _(sp):
            sp.dma_start(ids_sb[:, :], ids).then_inc(ids_loaded, 16)
            sp.dma_start(offsets_sb[:, :], offsets).then_inc(ids_loaded, 16)
            sp.dma_start(identity_sb[:, :], identity).then_inc(identity_loaded, 16)
            sp.dma_start(w0_raw[0], w0_upper).then_inc(w0_loaded, 16)
            sp.dma_start(w0_raw[1], w0_lower).then_inc(w0_loaded, 16)
            sp.dma_start(mask_sb[:, :], mask).then_inc(mask_loaded, 16)
            cols = FIELDS * CROSS // W1_PIECES
            for i in range(W1_PIECES):
                sp.dma_start(w1_raw[:, i * cols:(i + 1) * cols],
                             w1[:, i * cols:(i + 1) * cols]).then_inc(w1_loaded[i], 16)
            def load_later():
                sp.dma_start(w2_sb[:, :, :], w2).then_inc(w2_loaded, 16)
                for dst, src in ((wt1_sb[:, :, :], wt1), (wt1_context_sb[:, :], wt1_context),
                                 (wt2_sb[:, :, :], wt2), (wt3_sb[:, :], wt3), (bt1_sb[:, :], bt1),
                                 (bt2_sb[:, :], bt2), (dense_sb[:, :], dense)):
                    sp.dma_start(dst, src).then_inc(mlp_loaded, 16)

            def spread(s, par, pair):
                sp.wait_ge(gather_done[par], (pair + 1) * SPT * 16)
                sp.sem_inc(sp_waits_over, 1)
                wait(sp, x0_loaded, (s - 1) * 2 * GROUPS * 16)
                for j in range(GROUPS):
                    sp.dma_start(
                        scratch[par][:, :, j * P:(j + 1) * P].rearrange("w f r -> f w r"),
                        gathered[j * FIELDS:(j + 1) * FIELDS, par, :].unsqueeze(1).to_broadcast(
                            [FIELDS, 2, P])).then_inc(scratch_written[par], 16)
                sp.wait_ge(scratch_written[par], (pair + 1) * GROUPS * 16)
                sp.sem_inc(sp_waits_over, 1)
                wait(sp, pairs_ready, s * PAIR_CHUNKS)
                for j in range(GROUPS):
                    on = slice(j * FIELDS, (j + 1) * FIELDS)
                    chunks = -(-(SHIFTS - j) // GROUPS)
                    sp.dma_start(x0_rep[on, :], scratch[par][0, :, :]).then_inc(x0_loaded, 16)
                    shifted = bass.AP(tensor=scratch[par].tensor, offset=j * GROUPS * P,
                                      ap=[[GROUPS * P, FIELDS], [GROUPS * GROUPS * P, chunks],
                                          [1, GROUPS * P]])
                    sp.dma_start(x0_shifted[on, 0:chunks, :], shifted).then_inc(x0_loaded, 16)

            spread(0, 0, 0)
            load_later()
            spread(1, 1, 0)
            with sp.Fori(1, STEPS // 2) as k:
                spread(k * 2, 0, k)
                spread(k * 2 + 1, 1, k)
            sp.wait_ge(y_ready, 1)
            sp.dma_start(out, y_sb[:, :]).then_inc(out_written, 16)
            sp.wait_ge(out_written, 16)

        @block.gpsimd
        def _(gp):
            def take_rows(s, par, pair):
                wait(gp, gather_done[par], pair * SPT * 16)
                gp.sem_inc(waits_over, 1)
                nc.gpsimd.tensor_copy(rows_now[:, par, :],
                                      rows_sb[:, bass.ds(s * SPT, SPT)]).then_inc(rows_taken, 1)

            def gather(s, par, pair, which):
                gp.wait_ge(rows_taken, s + 1)
                wait(gp, transposed, s - 1)
                wait(gp, scratch_written[par], pair * GROUPS * 16)
                gp.sem_inc(waits_over, 1)
                for r in which:
                    nc.gpsimd.indirect_dma_start(
                        out=gathered[:, par, r * DIM:(r + 1) * DIM], out_offset=None, in_=table,
                        in_offset=bass.IndirectOffsetOnAxis(ap=rows_now[:, par, r:r + 1], axis=0),
                    ).then_inc(gather_done[par], 16)

            def diag(s, par, t):
                gp.wait_ge(rows_copied, s + 1)
                n, tp = s * GROUPS + t, (par * GROUPS + t) % 2
                wait(gp, s_made, n - 1)
                nc.gpsimd.tensor_tensor(
                    x0_diag[:, tp, :].rearrange("p (b f) -> p b f", f=FCOLS),
                    x0_rows[:, par, t, :].unsqueeze(1).to_broadcast([P, SPT, FCOLS]),
                    mask_sb[:, :].unsqueeze(2).to_broadcast([P, SPT, FCOLS]),
                    ALU.mult).then_inc(diag_ready, 1)

            def add(s, par, t, c):
                n, tp = s * GROUPS + t, (par * GROUPS + t) % 2
                width = chunk_fields(c) * CROSS
                gp.wait_ge(prod_ready, n * PRODUCTS + PRODUCTS_TO[c])
                wait(gp, g_op, n * G_OPS + G_OPS_TO[c] - 1)
                nc.gpsimd.tensor_tensor(acc_g[:, tp, 0:width], acc_g[:, tp, 0:width],
                                        prod[:, SLOT[c], 0:width], ALU.add).then_inc(g_op, 1)

            def fold(s, par, t):
                n, tp = s * GROUPS + t, (par * GROUPS + t) % 2
                gp.wait_ge(g_op, n * G_OPS + G_OPS - 1)
                nc.gpsimd.tensor_tensor(acc_g[:, tp, 0:2 * CROSS], acc_g[:, tp, 0:2 * CROSS],
                                        acc_g[:, tp, 2 * CROSS:4 * CROSS], ALU.add).then_inc(g_op, 1)
                gp.wait_ge(g_op, n * G_OPS + G_OPS)
                nc.gpsimd.tensor_tensor(acc_g[:, tp, 0:CROSS], acc_g[:, tp, 0:CROSS],
                                        acc_g[:, tp, CROSS:2 * CROSS], ALU.add).then_inc(acc_g_ready, 1)

            def step(s, par, pair):
                ahead = has(s, 2)
                if ahead:
                    take_rows(s + 2, par, pair + 1)
                for t in range(tiles_of(s)):
                    diag(s, par, t)
                    for i, c in enumerate(c for c in range(Y_CHUNKS) if KIND[c] == ADD_G):
                        if ahead and i < 2 and GATHERS_AT[t * 2 + i]:
                            gather(s + 2, par, pair + 1, GATHERS_AT[t * 2 + i])
                        add(s, par, t, c)
                    fold(s, par, t)

            gp.wait_ge(ids_loaded, 32)
            nc.gpsimd.tensor_tensor(rows_sb[:, :], ids_sb[:, :],
                                    offsets_sb[:, :].to_broadcast([GF, STEPS * SPT]),
                                    ALU.add).then_inc(rows_known, 1)
            gp.wait_ge(rows_known, 1)
            take_rows(0, 0, 0)
            gather(0, 0, 0, range(SPT))
            take_rows(1, 1, 0)
            gather(1, 1, 0, range(SPT))
            gp.wait_ge(mask_loaded, 16)
            gp.wait_ge(ones_set, 1)
            run_steps(gp, step)

        @block.scalar
        def _(act):
            def copy_rows(s, par):
                tiles = tiles_of(s)
                act.wait_ge(transposed, s + 1)
                wait(act, x2_ready, (s - 1) * GROUPS)
                wait(act, diag_ready, (s - 1) * GROUPS)
                nc.scalar.activation(
                    x0_rows[:, par, 0:tiles, 0:FIELDS],
                    rows_ps[:, 0:tiles * FIELDS].rearrange("p (t f) -> p t f", f=FIELDS),
                    ACT.Copy).then_inc(rows_copied, 1)

            def round_x1(s, par):
                width = tiles_of(s) * P
                act.wait_ge(pairs_used, (s + 1) * PAIR_CHUNKS)
                nc.scalar.activation(x1_hi[:, par, 0:width], x1_ps[:, 0:width],
                                     ACT.Copy).then_inc(x1_hi_ready, 1)

            def copy_s(s, t):
                n = s * GROUPS + t
                act.wait_ge(s_made, n + 1)
                nc.scalar.activation(
                    S[:, :, bass.ds(s * SPS + t * SPT, SPT)],
                    s_ps[:, 0:SPT * FCOLS].rearrange("p (b f) -> p f b", f=FCOLS),
                    ACT.Copy).then_inc(s_copied, 1)

            def multiply(s, par, t, c):
                n, tp = s * GROUPS + t, (par * GROUPS + t) % 2
                act.wait_ge(y_for_scalar, n * PRODUCTS + PRODUCTS_TO[c])
                if KIND[c] in (INIT_V, INIT_G):
                    wait(act, x2_ready, n - 1)
                    into = (acc_v if KIND[c] == INIT_V else acc_g)[:, tp, :]
                else:
                    if KIND[c] == ADD_V:
                        wait(act, v_op, (n - 1) * V_OPS + V_OPS_TO[c])
                    else:
                        wait(act, g_op, (n - 1) * G_OPS + G_OPS_TO[c])
                    into = prod[:, SLOT[c], :]
                for i in range(chunk_fields(c)):
                    f = c * YF + i
                    last = nc.scalar.activation(
                        into[:, i * CROSS:(i + 1) * CROSS],
                        y_bank(c)[:, i * CROSS:(i + 1) * CROSS], ACT.Copy,
                        scale=x0_rows[:, par, t, f:f + 1])
                last.then_inc(prod_ready, 1)

            def step(s, par, pair):
                act.wait_ge(rows_copied, s + 1)
                for t in range(tiles_of(s)):
                    for c in range(Y_CHUNKS):
                        at = t * Y_CHUNKS + c
                        if KIND[c] != MULT_V:
                            multiply(s, par, t, c)
                        if has(s, 1):
                            if at == AT_ROWS:
                                copy_rows(s + 1, 1 - par)
                            if at == AT_SUM[-1]:
                                round_x1(s + 1, 1 - par)
                        if c == AT_S:
                            if t > 0:
                                copy_s(s, t - 1)
                            elif not isinstance(s, int) or s > 0:
                                copy_s(s - 1, GROUPS - 1)

            act.wait_ge(ones_set, 1)
            copy_rows(0, 0)
            cols = FIELDS * CROSS // W1_PIECES
            for i in range(W1_PIECES):
                act.wait_ge(w1_loaded[i], 16)
                nc.scalar.activation(w1_hi[:, i * cols:(i + 1) * cols],
                                     w1_raw[:, i * cols:(i + 1) * cols],
                                     ACT.Copy).then_inc(w1_hi_ready, 1)
            round_x1(0, 0)
            run_steps(act, step)
            copy_s(STEPS - 1, LAST_TILES - 1)

            act.wait_ge(mlp_loaded, 7 * 16)
            for m in range(0, HIDDEN1 // P, 2):
                act.wait_ge(h1_made, m + 1)
                nc.scalar.activation(h1[:, m, :], h_ps[m][:, :], ACT.Relu,
                                     bias=bt1_sb[:, m:m + 1]).then_inc(h1_ready[0], 1)
            act.wait_ge(h2_made, 1)
            nc.scalar.activation(h2[:, 0, :], rows_ps[:, :], ACT.Relu,
                                 bias=bt2_sb[:, 0:1]).then_inc(h2_ready[0], 1)

        @block.vector
        def _(dve):
            def multiply_pairs(s, par, c):
                width, rows, i = tiles_of(s) * P, pair_rows(c), s * PAIR_CHUNKS + c
                buf = (par * PAIR_CHUNKS + c) % 2
                dve.wait_ge(x0_loaded, (s + 1) * 2 * GROUPS * 16)
                wait(dve, pairs_used, i - 1)
                nc.vector.tensor_tensor(pairs[0:rows, buf, 0:width], x0_rep[0:rows, 0:width],
                                        x0_shifted[0:rows, c, 0:width], ALU.mult).then_inc(pairs_ready, 1)

            def rest_of_x1(s, par):
                width = tiles_of(s) * P
                dve.wait_ge(x1_hi_ready, s + 1)
                nc.vector.tensor_tensor(x1_lo[:, par, 0:width], x1_ps[:, 0:width],
                                        x1_hi[:, par, 0:width], ALU.subtract).then_inc(x1_lo_ready, 1)

            def sum_x1(s, par):
                tiles = tiles_of(s)
                nc.vector.tensor_reduce(
                    r0[:, bass.ds(s * SPS, tiles * SPT)],
                    x1_ps[:, 0:tiles * P].rearrange("p (b d) -> p b d", d=DIM),
                    axis=AX.X, op=ALU.add).then_inc(r0_ready, 1)

            def accumulate(s, par, t, c):
                n, tp = s * GROUPS + t, (par * GROUPS + t) % 2
                before = n * V_OPS + (V_OPS_TO[c - 1] if c else 0)
                if KIND[c] == MULT_V:
                    dve.wait_ge(y_for_vector, n * (Y_CHUNKS - PRODUCTS) + c + 1 - PRODUCTS_TO[c])
                    for i in range(chunk_fields(c)):
                        f, lane = c * YF + i, acc_v[:, tp, i * CROSS:(i + 1) * CROSS]
                        if i == 0:
                            dve.wait_ge(prod_ready, n * PRODUCTS + PRODUCTS_TO[0])
                            wait(dve, v_op, before)
                        nc.vector.scalar_tensor_tensor(
                            lane, y_bank(c)[:, i * CROSS:(i + 1) * CROSS],
                            x0_rows[:, par, t, f:f + 1], lane, ALU.mult, ALU.add).then_inc(v_op, 1)
                else:
                    width = chunk_fields(c) * CROSS
                    dve.wait_ge(prod_ready, n * PRODUCTS + PRODUCTS_TO[c])
                    wait(dve, v_op, before)
                    nc.vector.tensor_tensor(acc_v[:, tp, 0:width], acc_v[:, tp, 0:width],
                                            prod[:, SLOT[c], 0:width], ALU.add).then_inc(v_op, 1)

            def fold(s, par, t):
                n, tp = s * GROUPS + t, (par * GROUPS + t) % 2
                dve.wait_ge(v_op, n * V_OPS + V_OPS - 2)
                nc.vector.tensor_tensor(acc_v[:, tp, 0:2 * CROSS], acc_v[:, tp, 0:2 * CROSS],
                                        acc_v[:, tp, 2 * CROSS:4 * CROSS], ALU.add).then_inc(v_op, 1)
                dve.wait_ge(v_op, n * V_OPS + V_OPS - 1)
                nc.vector.tensor_tensor(acc_v[:, tp, 0:CROSS], acc_v[:, tp, 0:CROSS],
                                        acc_v[:, tp, CROSS:2 * CROSS], ALU.add).then_inc(v_op, 1)
                dve.wait_ge(v_op, n * V_OPS + V_OPS)
                dve.wait_ge(acc_g_ready, n + 1)
                wait(dve, s_made, n - 1)
                nc.vector.tensor_tensor(x2[:, tp, :], acc_v[:, tp, 0:CROSS], acc_g[:, tp, 0:CROSS],
                                        ALU.add).then_inc(x2_ready, 1)

            def step(s, par, pair):
                dve.wait_ge(rows_copied, s + 1)
                for t in range(tiles_of(s)):
                    for c in range(Y_CHUNKS):
                        at = t * Y_CHUNKS + c
                        if KIND[c] in (MULT_V, ADD_V):
                            accumulate(s, par, t, c)
                        if has(s, 1):
                            if at in AT_MULTIPLY:
                                multiply_pairs(s + 1, 1 - par, AT_MULTIPLY.index(at))
                            if at == AT_SUM[-1]:
                                rest_of_x1(s + 1, 1 - par)
                            if at == AT_R0:
                                sum_x1(s + 1, 1 - par)
                    fold(s, par, t)

            nc.vector.memset(x0_rows[:, :, :, FIELDS:FCOLS], 1.0).then_inc(ones_set, 1)
            dve.wait_ge(w0_loaded, 32)
            nc.vector.tensor_tensor(w0[:, :], w0_raw[0], w0_raw[1], ALU.add).then_inc(w0_ready, 1)
            multiply_pairs(0, 0, 0)
            cols = FIELDS * CROSS // W1_PIECES
            for c in range(1, PAIR_CHUNKS):
                multiply_pairs(0, 0, c)
                if c % 2 == 0:
                    i = c // 2 - 1
                    dve.wait_ge(w1_hi_ready, i + 1)
                    nc.vector.tensor_tensor(w1_lo[:, i * cols:(i + 1) * cols],
                                            w1_raw[:, i * cols:(i + 1) * cols],
                                            w1_hi[:, i * cols:(i + 1) * cols],
                                            ALU.subtract).then_inc(w1_lo_ready, 1)
            rest_of_x1(0, 0)
            sum_x1(0, 0)
            run_steps(dve, step)

            dve.wait_ge(r2_made, 1)
            nc.vector.tensor_copy(r2[:, :], r2_ps[:, :]).then_inc(r2_ready, 1)
            dve.wait_ge(mlp_loaded, 7 * 16)
            for m in range(1, HIDDEN1 // P, 2):
                dve.wait_ge(h1_made, m + 1)
                nc.vector.tensor_scalar(h1[:, m, :], h_ps[m][:, :], bt1_sb[:, m:m + 1], 0.0,
                                        ALU.add, ALU.max).then_inc(h1_ready[1], 1)
            dve.wait_ge(h2_made, 2)
            nc.vector.tensor_scalar(h2[:, 1, :], x1_ps[:, :], bt2_sb[:, 1:2], 0.0,
                                    ALU.add, ALU.max).then_inc(h2_ready[1], 1)
            dve.wait_ge(y_made, 1)
            nc.vector.tensor_copy(y_sb[:, :], s_ps[0:1, :]).then_inc(y_ready, 1)

        @block.tensor
        def _(pe):
            mm = nc.tensor.matmul

            def transpose_rows(s, par, pair):
                pe.wait_ge(gather_done[par], (pair + 1) * SPT * 16)
                wait(pe, rows_copied, s)
                nc.tensor.transpose(rows_ps[:, 0:GF], gathered[:, par, :],
                                    identity_sb[:, :]).then_inc(transposed, 1)

            def sum_pairs(s, par, c):
                width, rows, i = tiles_of(s) * P, pair_rows(c), s * PAIR_CHUNKS + c
                pe.wait_ge(pairs_ready, i + 1)
                if c == 0:
                    wait(pe, r0_ready, s)
                mm(x1_ps[:, 0:width], w0[0:rows, c * CROSS:(c + 1) * CROSS],
                   pairs[0:rows, (par * PAIR_CHUNKS + c) % 2, 0:width],
                   start=c == 0, stop=c == PAIR_CHUNKS - 1).then_inc(pairs_used, 1)

            def y_chunk(s, par, t, c):
                n, width = s * GROUPS + t, chunk_fields(c) * CROSS
                if c >= Y_BANKS:
                    wait_chunk_used(pe, c - Y_BANKS, n)
                elif not isinstance(n, int) or n > 0:
                    wait_chunk_used(pe, c + Y_CHUNKS - Y_BANKS, n - 1)
                y = y_bank(c)[:, 0:width]
                w = slice(c * YF * CROSS, c * YF * CROSS + width)
                hi, lo = x1_hi[:, par, t * P:(t + 1) * P], x1_lo[:, par, t * P:(t + 1) * P]
                mm(y, hi, w1_hi[:, w], start=True, stop=False)
                mm(y, hi, w1_lo[:, w], start=False, stop=False)
                mm(y, lo, w1_hi[:, w], start=False, stop=True).then_inc(
                    y_for_vector if KIND[c] == MULT_V else y_for_scalar, 1)

            def make_s(s, par, t):
                n, tp = s * GROUPS + t, (par * GROUPS + t) % 2
                pe.wait_ge(x2_ready, n + 1)
                pe.wait_ge(diag_ready, n + 1)
                wait(pe, s_copied, n)
                mm(s_ps[:, 0:SPT * FCOLS], x2[:, tp, :], x0_diag[:, tp, :],
                   start=True, stop=True).then_inc(s_made, 1)

            def step(s, par, pair):
                pe.wait_ge(x1_hi_ready, s + 1)
                pe.wait_ge(x1_lo_ready, s + 1)
                if isinstance(s, int) and s == 0:
                    pe.wait_ge(w1_lo_ready, W1_PIECES)
                for t in range(tiles_of(s)):
                    for c in range(Y_CHUNKS):
                        at = t * Y_CHUNKS + c
                        y_chunk(s, par, t, c)
                        if has(s, 1):
                            if at == AT_ROWS:
                                transpose_rows(s + 1, 1 - par, pair + par)
                            if at in AT_SUM:
                                sum_pairs(s + 1, 1 - par, AT_SUM.index(at))
                        if c == AT_S:
                            if t > 0:
                                make_s(s, par, t - 1)
                            elif not isinstance(s, int) or s > 0:
                                make_s(s - 1, 1 - par, GROUPS - 1)

            pe.wait_ge(identity_loaded, 16)
            transpose_rows(0, 0, 0)
            pe.wait_ge(w0_ready, 1)
            for c in range(PAIR_CHUNKS):
                sum_pairs(0, 0, c)
            run_steps(pe, step)
            make_s(STEPS - 1, 1, LAST_TILES - 1)

            last_tile = TILES - 1
            pe.wait_ge(prod_ready, (last_tile + 1) * PRODUCTS)
            pe.wait_ge(v_op, (last_tile + 1) * V_OPS)
            pe.wait_ge(mlp_loaded, 7 * 16)
            pe.wait_ge(r0_ready, STEPS)
            pe.wait_ge(s_copied, TILES)
            for m in range(HIDDEN1 // P):
                units = slice(m * P, (m + 1) * P)
                mm(h_ps[m][:, :], wt1_sb[:, 0, units], r0[:, :], start=True, stop=False)
                mm(h_ps[m][:, :], wt1_sb[:, 1, units], S[:, FIELDS, :], start=False, stop=False)
                mm(h_ps[m][:, :], wt1_context_sb[:, units], dense_sb[:, :], start=False, stop=False)
            pe.wait_ge(w2_loaded, 16)
            for f in range(FIELDS):
                last = mm(r2_ps[:, :], w2_sb[:, f, :], S[:, f, :], start=f == 0, stop=f == FIELDS - 1)
            last.then_inc(r2_made, 1)
            pe.wait_ge(r2_ready, 1)
            for m in range(HIDDEN1 // P):
                mm(h_ps[m][:, :], wt1_sb[:, 2, m * P:(m + 1) * P], r2[:, :],
                   start=False, stop=True).then_inc(h1_made, 1)
            for k in range(HIDDEN1 // P):
                pe.wait_ge(h1_ready[k % 2], k // 2 + 1)
                for m in range(HIDDEN2 // P):
                    last = mm((rows_ps, x1_ps)[m][:, :], wt2_sb[:, k, m * P:(m + 1) * P], h1[:, k, :],
                              start=k == 0, stop=k == HIDDEN1 // P - 1)
                    if k == HIDDEN1 // P - 1:
                        last.then_inc(h2_made, 1)
            for m in range(HIDDEN2 // P):
                pe.wait_ge(h2_ready[m], 1)
                last = mm(s_ps[0:1, :], wt3_sb[:, m:m + 1], h2[:, m, :],
                          start=m == 0, stop=m == HIDDEN2 // P - 1)
            last.then_inc(y_made, 1)


def pair_layout(w0):
    w0 = w0.reshape(FIELDS, FIELDS, CROSS)
    upper = np.zeros((GF, PAIR_CHUNKS, CROSS), np.float32)
    lower = np.zeros((GF, PAIR_CHUNKS, CROSS), np.float32)
    f = np.arange(FIELDS)
    for s in range(SHIFTS):
        rows = slice(s % GROUPS * FIELDS, (s % GROUPS + 1) * FIELDS)
        upper[rows, s // GROUPS] = w0[f, (f + s) % FIELDS]
        if s:
            lower[rows, s // GROUPS] = w0[(f + s) % FIELDS, f]
    return upper.reshape(GF, -1), lower.reshape(GF, -1)


def kernel(**inputs):
    import concourse.bacc as bacc
    from concourse.bass_utils import run_bass_kernel_spmd

    x = {k: np.asarray(v) for k, v in inputs.items()}
    tables = [x[f"tbl_{i}"] for i in range(FIELDS)]
    sizes = [t.shape[0] for t in tables]
    starts = np.concatenate([[0], np.cumsum(sizes)[:-1]]).astype(np.int32)
    ids = np.zeros((STEPS * SPS, FIELDS), np.int32)
    ids[:BATCH] = x["ids"]
    ids = ids.reshape(STEPS, GROUPS, SPT, FIELDS).transpose(1, 3, 0, 2).reshape(GF, STEPS * SPT)
    mask = np.zeros((P, SPT), np.float32)
    mask[np.arange(P), np.arange(P) // DIM] = 1
    upper, lower = pair_layout(x["L0_rec_f0"])

    def by_g(w):
        return w.reshape(FIELDS, CROSS, CROSS).transpose(1, 0, 2)

    wt1 = x["W_top1"]
    arrays = {
        "in_ids": ids,
        "in_offsets": np.tile(starts, GROUPS)[:, None],
        "in_table": np.concatenate(tables, axis=0),
        "in_identity": np.eye(GF, dtype=np.float32),
        "in_mask": mask,
        "in_w0_upper": upper,
        "in_w0_lower": lower,
        "in_w1": by_g(x["L0_rec_f1"]).reshape(P, FIELDS * CROSS),
        "in_w2": by_g(x["L0_rec_f2"]),
        "in_dense": x["dense_ctx"].T,
        "in_wt1": wt1[:3 * P].reshape(3, P, HIDDEN1).transpose(1, 0, 2),
        "in_wt1_context": wt1[3 * P:],
        "in_bt1": x["b_top1"].reshape(-1, P).T,
        "in_wt2": x["W_top2"].reshape(-1, P, HIDDEN2).transpose(1, 0, 2),
        "in_bt2": x["b_top2"].reshape(-1, P).T,
        "in_wt3": x["W_top3"].reshape(-1, P).T,
    }
    arrays = {k: np.ascontiguousarray(v) for k, v in arrays.items()}
    nc = bacc.Bacc("TRN2", target_bir_lowering=False, num_devices=1)
    args = [nc.dram_tensor(k, v.shape, mybir.dt.from_np(v.dtype), kind="ExternalInput").ap()
            for k, v in arrays.items()]
    out = nc.dram_tensor("out_y", (1, BATCH), mybir.dt.float32, kind="ExternalOutput").ap()
    program(nc, *args, out)
    r = run_bass_kernel_spmd(nc, [arrays], core_ids=[0])
    return r.results[0]["out_y"].reshape(BATCH, 1)
```

```python
from contextlib import ExitStack

import numpy as np

import concourse.bass as bass
from concourse import mybir

BATCH, FIELDS, DIM, CROSS, CONTEXT = 512, 39, 16, 128, 16
HIDDEN1, HIDDEN2 = 512, 256
P = 128
GROUPS = P // FIELDS
GF = GROUPS * FIELDS
SPT = P // DIM
SPS = SPT * GROUPS
TILES = BATCH // SPT
STEPS = -(-TILES // GROUPS)
LAST_TILES = TILES - (STEPS - 1) * GROUPS
SHIFTS = (FIELDS + 1) // 2
PAIR_CHUNKS = -(-SHIFTS // GROUPS)
FCOLS = FIELDS + 1
YF = 4
Y_CHUNKS = -(-FIELDS // YF)
Y_BANKS = 5
W1_PIECES = 3
FIRST_CHUNKS = 3
WARM_UP = 26
S_BUFS = (PAIR_CHUNKS + 1) * GROUPS * P // BATCH
W2_FIELDS = 3
W2_LOADS = [0, 2, 6, FIELDS // W2_FIELDS]

INIT_V, INIT_G, MULT_V, ADD_V, ADD_G = range(5)
KIND = [INIT_V, INIT_G, MULT_V, ADD_V, ADD_G, MULT_V, ADD_V, ADD_G, MULT_V, ADD_V]
SLOT = {c: i for i, c in enumerate(c for c in range(Y_CHUNKS) if KIND[c] in (ADD_V, ADD_G))}


def chunk_fields(c):
    return min(YF, FIELDS - c * YF)


PRODUCTS = sum(k != MULT_V for k in KIND)
PRODUCTS_TO = [sum(k != MULT_V for k in KIND[:c + 1]) for c in range(Y_CHUNKS)]
V_STEPS = [chunk_fields(c) if KIND[c] == MULT_V else 2 if KIND[c] == ADD_V else 0
           for c in range(Y_CHUNKS)]
V_OPS_TO = [sum(V_STEPS[:c + 1]) for c in range(Y_CHUNKS)]
V_OPS = V_OPS_TO[-1]
G_OPS_TO = [sum(k == ADD_G for k in KIND[:c + 1]) for c in range(Y_CHUNKS)]
G_OPS = G_OPS_TO[-1] + 1

AT_ROWS = 2
AT_MULTIPLY = [2, 3, 5, 8, 11, 14, 17]
AT_SUM = [7, 10, 13, 16, 19, 22, 25]
AT_R0 = 29
SPLIT_CHUNKS = [3, 4, 5, 6]
AT_ROUND = [10, 13, 16, 19]
AT_REST = [11, 14, 17, 20]
PAIR_BUFS = 3
GATHERS_AT = [(0, 1, 2), (3,), (4, 5, 6), (7,), (), ()]
AT_FOLD, AT_X2 = 2, 3
AT_S = 8


def program(nc, ids, offsets, table, identity, mask, w0_upper, w0_lower, w1, w2, dense, wt1,
            wt1_context, bt1, wt2, bt2, wt3, out):
    f32, f32r, i32 = mybir.dt.float32, mybir.dt.float32r, mybir.dt.int32
    ALU, ACT, AX = mybir.AluOpType, mybir.ActivationFunctionType, mybir.AxisListType
    ctx = ExitStack()
    with ctx:
        def sb(name, shape, dtype):
            return ctx.enter_context(nc.sbuf_tensor(name, shape, dtype))

        def ps(name):
            return ctx.enter_context(nc.psum_tensor(name, [P, 512], f32))

        def sem(name):
            return ctx.enter_context(nc.semaphore(name))

        ids_sb = sb("ids_sb", [GF, STEPS * SPT], i32)
        rows_sb = sb("rows_sb", [GF, STEPS * SPT], i32)
        offsets_sb = sb("offsets_sb", [GF, 1], i32)
        identity_sb = sb("identity_sb", [GF, GF], f32)
        mask_sb = sb("mask_sb", [P, SPT], f32)
        w0 = sb("w0", [GF, PAIR_CHUNKS * CROSS], f32)
        w0_hi = sb("w0_hi", [GF, PAIR_CHUNKS * CROSS], f32r)
        w0_lo = sb("w0_lo", [GF, PAIR_CHUNKS * CROSS], f32r)
        pairs_hi = sb("pairs_hi", [GF, PAIR_BUFS, GROUPS * P], f32r)
        with ExitStack() as until_rounded:
            pairs = until_rounded.enter_context(
                nc.sbuf_tensor("pairs", [GF, PAIR_BUFS, GROUPS * P], f32))
        pairs_lo = sb("pairs_lo", [GF, PAIR_BUFS, GROUPS * P], f32r)
        w1_hi = sb("w1_hi", [P, FIELDS * CROSS], f32r)
        with ExitStack() as until_layer_2:
            w1_lo = until_layer_2.enter_context(
                nc.sbuf_tensor("w1_lo", [P, FIELDS * CROSS], f32r))
        with ExitStack() as until_w2_rounded:
            w2_raw = until_w2_rounded.enter_context(
                nc.sbuf_tensor("w2_raw", [P, FIELDS * CROSS], f32))
        w2_lo = sb("w2_lo", [P, FIELDS * CROSS], f32r)
        w2_hi = w1_hi
        wt1_sb = sb("wt1_sb", [P, 3, HIDDEN1], f32)
        wt1_context_sb = sb("wt1_context_sb", [CONTEXT, HIDDEN1], f32)
        wt2_sb = sb("wt2_sb", [P, HIDDEN1 // P, HIDDEN2], f32)
        wt3_sb = sb("wt3_sb", [P, HIDDEN2 // P], f32)
        bt1_sb = sb("bt1_sb", [P, HIDDEN1 // P], f32)
        bt2_sb = sb("bt2_sb", [P, HIDDEN2 // P], f32)
        dense_sb = sb("dense_sb", [CONTEXT, BATCH], f32)
        rows_now = sb("rows_now", [GF, 2, SPT], i32)
        gathered = sb("gathered", [GF, 2, P], f32)
        x0_rows = sb("x0_rows", [P, 2, GROUPS, FCOLS], f32)
        x0_diag = sb("x0_diag", [P, 2, SPT * FCOLS], f32)
        x1_hi = sb("x1_hi", [P, 2, GROUPS * P], f32r)
        x1_lo = sb("x1_lo", [P, 2, GROUPS * P], f32r)
        prod = sb("prod", [P, len(SLOT), YF * CROSS], f32)
        acc_v = sb("acc_v", [P, 2, YF * CROSS], f32)
        acc_g = sb("acc_g", [P, 2, YF * CROSS], f32)
        x2 = sb("x2", [P, 2, CROSS], f32)
        r0 = sb("r0", [P, BATCH], f32)
        r2 = sb("r2", [P, BATCH], f32)
        with ExitStack() as until_rounded:
            S = until_rounded.enter_context(nc.sbuf_tensor("S", [P, FCOLS, BATCH], f32))
        s_lo = sb("s_lo", [P, FCOLS, BATCH], f32r)
        S_flat = S[:, :, :].rearrange("p f b -> p (f b)")
        w1_raw = S_flat[:, 0:FIELDS * CROSS]
        w0_raw = [S_flat[0:GF, 10 * BATCH + i * PAIR_CHUNKS * CROSS:
                         10 * BATCH + (i + 1) * PAIR_CHUNKS * CROSS] for i in range(2)]
        with ExitStack() as early:
            def sb_early(name, shape, dtype):
                return early.enter_context(nc.sbuf_tensor(name, shape, dtype))

            x0_shifted = sb_early("x0_shifted", [GF, PAIR_CHUNKS * GROUPS * P], f32)
            x0_rep = sb_early("x0_rep", [GF, GROUPS * P], f32)
        s_hi = sb("s_hi", [P, S_BUFS, BATCH], f32r)
        h1 = prod[:, 0:HIDDEN1 // P, :]
        h2 = acc_v
        y_sb = r2[0:1, :]

        y_ps = [ps(f"y_ps{i}") for i in range(Y_BANKS)]
        rows_ps = ps("rows_ps")
        x1_ps = ps("x1_ps")
        s_ps = ps("s_ps")

        h_ps, h2_ps, r2_ps = [rows_ps, x1_ps, y_ps[1], y_ps[2]], y_ps[3:], y_ps[0]
        scratch = [nc.dram_tensor(f"x0_scratch{i}", [2, FIELDS, GROUPS * P], f32).ap()
                   for i in range(2)]

        ids_loaded, w0_loaded = sem("ids_loaded"), sem("w0_loaded")
        identity_loaded = sem("identity_loaded")
        w1_loaded = [sem(f"w1_loaded{i}") for i in range(W1_PIECES)]
        mask_loaded, mlp_loaded = sem("mask_loaded"), sem("mlp_loaded")
        w2_loaded = [sem(f"w2_loaded{i}") for i in range(len(W2_LOADS) - 1)]
        rows_known = sem("rows_known")
        rows_taken = sem("rows_taken")
        gather_done = [sem("gather_done0"), sem("gather_done1")]
        waits_over = sem("waits_over")
        sp_waits_over = sem("sp_waits_over")
        scratch_written = [sem("scratch_written0"), sem("scratch_written1")]
        x0_loaded = sem("x0_loaded")
        x0_first_loaded = sem("x0_first_loaded")
        diag_ready = sem("diag_ready")
        g_op = sem("g_op")
        acc_g_ready = sem("acc_g_ready")
        ones_set = sem("ones_set")
        w0_ready = sem("w0_ready")
        w0_hi_ready, w0_lo_ready = sem("w0_hi_ready"), sem("w0_lo_ready")
        w1_hi_ready = sem("w1_hi_ready")
        w1_lo_ready = sem("w1_lo_ready")
        transposed = sem("transposed")
        rows_copied = sem("rows_copied")
        pairs_ready = sem("pairs_ready")
        pairs_hi_ready = sem("pairs_hi_ready")
        pairs_lo_ready = sem("pairs_lo_ready")
        pairs_used = sem("pairs_used")
        x1_hi_ready = sem("x1_hi_ready")
        x1_lo_ready = sem("x1_lo_ready")
        r0_ready = sem("r0_ready")
        y_for_scalar, y_for_vector = sem("y_for_scalar"), sem("y_for_vector")
        prod_ready = sem("prod_ready")
        v_op = sem("v_op")
        folded = sem("folded")
        x2_ready = sem("x2_ready")
        s_made = sem("s_made")
        s_copied = sem("s_copied")
        s_hi_ready, s_lo_ready = sem("s_hi_ready"), sem("s_lo_ready")
        w2_hi_ready, w2_lo_ready = sem("w2_hi_ready"), sem("w2_lo_ready")
        s_used = sem("s_used")
        r2_made, r2_ready = sem("r2_made"), sem("r2_ready")
        h1_made, h2_made, y_made = sem("h1_made"), sem("h2_made"), sem("y_made")
        h1_ready = [sem("h1_by_scalar"), sem("h1_by_vector")]
        h2_ready = [sem("h2_by_scalar"), sem("h2_by_vector")]
        y_ready, out_written = sem("y_ready"), sem("out_written")

        def loads_to(s):
            return (s + 1) * 2 * 16 - 16

        def split_count(s, c):
            return (s - 1) * len(SPLIT_CHUNKS) + SPLIT_CHUNKS.index(c) + 1

        def pair_rows(c):
            return FIELDS * len(range(c, SHIFTS, PAIR_CHUNKS))

        def wait(engine, semaphore, value):
            if not isinstance(value, int) or value > 0:
                engine.wait_ge(semaphore, value)

        def y_bank(c):
            return y_ps[c % Y_BANKS]

        def wait_chunk_used(engine, c, n):
            if KIND[c] == MULT_V:
                wait(engine, v_op, n * V_OPS + V_OPS_TO[c])
            else:
                wait(engine, prod_ready, n * PRODUCTS + PRODUCTS_TO[c])

        def tiles_of(s):
            return LAST_TILES if isinstance(s, int) and s == STEPS - 1 else GROUPS

        def has(s, ahead):
            return not isinstance(s, int) or s + ahead < STEPS

        def run_steps(engine, step):
            step(0, 0, 0)
            step(1, 1, 0)
            with engine.Fori(1, STEPS // 2 - 1) as k:
                step(k * 2, 0, k)
                step(k * 2 + 1, 1, k)
            step(STEPS - 2, 0, STEPS // 2 - 1)
            step(STEPS - 1, 1, STEPS // 2 - 1)

        block = ctx.enter_context(nc.Block())

        @block.sync
        def _(sp):
            sp.dma_start(ids_sb[:, :], ids).then_inc(ids_loaded, 16)
            sp.dma_start(offsets_sb[:, :], offsets).then_inc(ids_loaded, 16)
            sp.dma_start(identity_sb[:, :], identity).then_inc(identity_loaded, 16)
            sp.dma_start(w0_raw[0], w0_upper).then_inc(w0_loaded, 16)
            sp.dma_start(w0_raw[1], w0_lower).then_inc(w0_loaded, 16)
            sp.dma_start(mask_sb[:, :], mask).then_inc(mask_loaded, 16)
            cols = FIELDS * CROSS // W1_PIECES
            for i in range(W1_PIECES):
                sp.dma_start(w1_raw[:, i * cols:(i + 1) * cols],
                             w1[:, i * cols:(i + 1) * cols]).then_inc(w1_loaded[i], 16)

            def load_later():
                for dst, src in ((wt1_sb[:, :, :], wt1), (wt1_context_sb[:, :], wt1_context),
                                 (wt2_sb[:, :, :], wt2), (wt3_sb[:, :], wt3), (bt1_sb[:, :], bt1),
                                 (bt2_sb[:, :], bt2), (dense_sb[:, :], dense)):
                    sp.dma_start(dst, src).then_inc(mlp_loaded, 16)

            def spread(s, par, pair):
                sp.wait_ge(gather_done[par], (pair + 1) * SPT * 16)
                sp.sem_inc(sp_waits_over, 1)
                if not isinstance(s, int) or s > 1:
                    sp.wait_ge(x0_loaded, loads_to(s - 2))
                for w in range(2):
                    written = bass.AP(tensor=scratch[par].tensor, offset=w * FIELDS * GROUPS * P,
                                      ap=[[P, GROUPS], [GROUPS * P, FIELDS], [1, P]])
                    sp.dma_start(written, gathered[:, par, :]).then_inc(scratch_written[par], 16)
                sp.wait_ge(scratch_written[par], (pair + 1) * 2 * 16)
                sp.sem_inc(sp_waits_over, 1)
                wait(sp, pairs_ready, s * PAIR_CHUNKS)
                first = isinstance(s, int) and s == 0
                repeated = bass.AP(tensor=scratch[par].tensor, offset=0,
                                   ap=[[0, GROUPS], [GROUPS * P, FIELDS], [1, GROUPS * P]])
                sp.dma_start(x0_rep[:, :], repeated).then_inc(
                    x0_first_loaded if first else x0_loaded, 16)
                for begin, end in ((0, FIRST_CHUNKS), (FIRST_CHUNKS, PAIR_CHUNKS)) if first else (
                        (0, PAIR_CHUNKS),):
                    shifted = bass.AP(
                        tensor=scratch[par].tensor, offset=begin * GROUPS * P,
                        ap=[[PAIR_CHUNKS * GROUPS * P, GROUPS], [GROUPS * P, FIELDS],
                            [1, (end - begin) * GROUPS * P]])
                    sp.dma_start(x0_shifted[:, begin * GROUPS * P:end * GROUPS * P], shifted).then_inc(
                        x0_first_loaded if first and begin == 0 else x0_loaded, 16)

            spread(0, 0, 0)
            spread(1, 1, 0)
            load_later()
            with sp.Fori(1, STEPS // 2) as k:
                spread(k * 2, 0, k)
                spread(k * 2 + 1, 1, k)
            sp.wait_ge(y_for_scalar, TILES * PRODUCTS)
            sp.wait_ge(y_for_vector, TILES * (Y_CHUNKS - PRODUCTS))
            for i in range(len(W2_LOADS) - 1):
                cols = slice(W2_LOADS[i] * W2_FIELDS * CROSS, W2_LOADS[i + 1] * W2_FIELDS * CROSS)
                sp.dma_start(w2_raw[:, cols], w2[:, cols]).then_inc(w2_loaded[i], 16)
            sp.wait_ge(y_ready, 1)
            sp.dma_start(out, y_sb[:, :]).then_inc(out_written, 16)
            sp.wait_ge(out_written, 16)

        @block.gpsimd
        def _(gp):
            def take_rows(s, par, pair):
                wait(gp, gather_done[par], pair * SPT * 16)
                gp.sem_inc(waits_over, 1)
                nc.gpsimd.tensor_copy(rows_now[:, par, :],
                                      rows_sb[:, bass.ds(s * SPT, SPT)]).then_inc(rows_taken, 1)

            def gather(s, par, pair, which):
                gp.wait_ge(rows_taken, s + 1)
                wait(gp, transposed, s - 1)
                wait(gp, scratch_written[par], pair * 2 * 16)
                gp.sem_inc(waits_over, 1)
                for r in which:
                    nc.gpsimd.indirect_dma_start(
                        out=gathered[:, par, r * DIM:(r + 1) * DIM], out_offset=None, in_=table,
                        in_offset=bass.IndirectOffsetOnAxis(ap=rows_now[:, par, r:r + 1], axis=0),
                    ).then_inc(gather_done[par], 16)

            def diag(s, par, t):
                gp.wait_ge(rows_copied, s + 1)
                n, tp = s * GROUPS + t, (par * GROUPS + t) % 2
                wait(gp, s_made, n - 1)
                nc.gpsimd.tensor_tensor(
                    x0_diag[:, tp, :].rearrange("p (b f) -> p b f", f=FCOLS),
                    x0_rows[:, par, t, :].unsqueeze(1).to_broadcast([P, SPT, FCOLS]),
                    mask_sb[:, :].unsqueeze(2).to_broadcast([P, SPT, FCOLS]),
                    ALU.mult).then_inc(diag_ready, 1)

            def add(s, par, t, c):
                n, tp = s * GROUPS + t, (par * GROUPS + t) % 2
                width = chunk_fields(c) * CROSS
                gp.wait_ge(prod_ready, n * PRODUCTS + PRODUCTS_TO[c])
                wait(gp, g_op, n * G_OPS + G_OPS_TO[c] - 1)
                nc.gpsimd.tensor_tensor(acc_g[:, tp, 0:width], acc_g[:, tp, 0:width],
                                        prod[:, SLOT[c], 0:width], ALU.add).then_inc(g_op, 1)

            def fold(s, par, t):
                n, tp = s * GROUPS + t, (par * GROUPS + t) % 2
                gp.wait_ge(g_op, n * G_OPS + G_OPS - 1)
                nc.gpsimd.tensor_tensor(acc_g[:, tp, 0:2 * CROSS], acc_g[:, tp, 0:2 * CROSS],
                                        acc_g[:, tp, 2 * CROSS:4 * CROSS], ALU.add).then_inc(g_op, 1)
                gp.wait_ge(g_op, n * G_OPS + G_OPS)
                nc.gpsimd.tensor_tensor(acc_g[:, tp, 0:CROSS], acc_g[:, tp, 0:CROSS],
                                        acc_g[:, tp, CROSS:2 * CROSS], ALU.add).then_inc(acc_g_ready, 1)

            def step(s, par, pair):
                ahead = has(s, 2)
                if ahead:
                    take_rows(s + 2, par, pair + 1)
                for t in range(tiles_of(s)):
                    diag(s, par, t)
                    for i, c in enumerate(c for c in range(Y_CHUNKS) if KIND[c] == ADD_G):
                        if ahead and i < 2 and GATHERS_AT[t * 2 + i]:
                            gather(s + 2, par, pair + 1, GATHERS_AT[t * 2 + i])
                        add(s, par, t, c)
                    fold(s, par, t)

            gp.wait_ge(ids_loaded, 32)
            nc.gpsimd.tensor_tensor(rows_sb[:, :], ids_sb[:, :],
                                    offsets_sb[:, :].to_broadcast([GF, STEPS * SPT]),
                                    ALU.add).then_inc(rows_known, 1)
            gp.wait_ge(rows_known, 1)
            take_rows(0, 0, 0)
            gather(0, 0, 0, range(SPT))
            take_rows(1, 1, 0)
            gather(1, 1, 0, range(SPT))
            gp.wait_ge(mask_loaded, 16)
            gp.wait_ge(ones_set, 1)
            run_steps(gp, step)

            for i in range(FIELDS // W2_FIELDS):
                cols = slice(i * W2_FIELDS * CROSS, (i + 1) * W2_FIELDS * CROSS)
                gp.wait_ge(w2_hi_ready, i + 1)
                nc.gpsimd.tensor_tensor(
                    w2_lo[:, cols], w2_raw[:, cols],
                    w2_hi[:, cols], ALU.subtract).then_inc(w2_lo_ready, 1)

        @block.scalar
        def _(act):
            def copy_rows(s, par):
                tiles = tiles_of(s)
                act.wait_ge(transposed, s + 1)
                wait(act, v_op, (s - 1) * GROUPS * V_OPS)
                wait(act, diag_ready, (s - 1) * GROUPS)
                nc.scalar.activation(
                    x0_rows[:, par, 0:tiles, 0:FIELDS],
                    rows_ps[:, 0:tiles * FIELDS].rearrange("p (t f) -> p t f", f=FIELDS),
                    ACT.Copy).then_inc(rows_copied, 1)

            def round_pairs(s, c):
                width, rows, buf = tiles_of(s) * P, pair_rows(c), c % PAIR_BUFS
                act.wait_ge(pairs_ready, s * PAIR_CHUNKS + c + 1)
                nc.scalar.activation(pairs_hi[0:rows, buf, 0:width], pairs[0:rows, buf, 0:width],
                                     ACT.Copy).then_inc(pairs_hi_ready, 1)

            def round_x1(s, par):
                width = tiles_of(s) * P
                act.wait_ge(pairs_used, (s + 1) * PAIR_CHUNKS)
                nc.scalar.activation(x1_hi[:, par, 0:width], x1_ps[:, 0:width],
                                     ACT.Copy).then_inc(x1_hi_ready, 1)

            def copy_s(s, t):
                n = s * GROUPS + t
                act.wait_ge(s_made, n + 1)
                nc.scalar.activation(
                    S[:, :, bass.ds(s * SPS + t * SPT, SPT)],
                    s_ps[:, 0:SPT * FCOLS].rearrange("p (b f) -> p f b", f=FCOLS),
                    ACT.Copy).then_inc(s_copied, 1)

            def multiply(s, par, t, c):
                n, tp = s * GROUPS + t, (par * GROUPS + t) % 2
                act.wait_ge(y_for_scalar, n * PRODUCTS + PRODUCTS_TO[c])
                if KIND[c] in (INIT_V, INIT_G):
                    wait(act, x2_ready, n - 1)
                    into = (acc_v if KIND[c] == INIT_V else acc_g)[:, tp, :]
                else:
                    if KIND[c] == ADD_V:
                        wait(act, v_op, (n - 1) * V_OPS + V_OPS_TO[c])
                    else:
                        wait(act, g_op, (n - 1) * G_OPS + G_OPS_TO[c])
                    into = prod[:, SLOT[c], :]
                for i in range(chunk_fields(c)):
                    f = c * YF + i
                    last = nc.scalar.activation(
                        into[:, i * CROSS:(i + 1) * CROSS],
                        y_bank(c)[:, i * CROSS:(i + 1) * CROSS], ACT.Copy,
                        scale=x0_rows[:, par, t, f:f + 1])
                last.then_inc(prod_ready, 1)

            def step(s, par, pair):
                act.wait_ge(rows_copied, s + 1)
                for t in range(tiles_of(s)):
                    for c in range(Y_CHUNKS):
                        at = t * Y_CHUNKS + c
                        if KIND[c] != MULT_V:
                            multiply(s, par, t, c)
                        if has(s, 1):
                            if at == AT_ROWS:
                                copy_rows(s + 1, 1 - par)
                            if at in AT_ROUND:
                                round_pairs(s + 1, SPLIT_CHUNKS[AT_ROUND.index(at)])
                            if at == AT_SUM[-1]:
                                round_x1(s + 1, 1 - par)
                        if c == AT_S:
                            if t > 0:
                                copy_s(s, t - 1)
                            elif not isinstance(s, int) or s > 0:
                                copy_s(s - 1, GROUPS - 1)

            cols = FIELDS * CROSS // W1_PIECES
            for i in range(W1_PIECES):
                act.wait_ge(w1_loaded[i], 16)
                nc.scalar.activation(w1_hi[:, i * cols:(i + 1) * cols],
                                     w1_raw[:, i * cols:(i + 1) * cols],
                                     ACT.Copy).then_inc(w1_hi_ready, 1)
            act.wait_ge(w0_ready, 1)
            nc.scalar.activation(w0_hi[:, :], w0[:, :], ACT.Copy).then_inc(w0_hi_ready, 1)
            act.wait_ge(ones_set, 1)
            copy_rows(0, 0)
            round_x1(0, 0)
            run_steps(act, step)

            def round_w2(i):
                cols = slice(i * W2_FIELDS * CROSS, (i + 1) * W2_FIELDS * CROSS)
                if i in W2_LOADS:
                    act.wait_ge(w2_loaded[W2_LOADS.index(i)], 16)
                nc.scalar.activation(w2_hi[:, cols], w2_raw[:, cols],
                                     ACT.Copy).then_inc(w2_hi_ready, 1)

            copy_s(STEPS - 1, LAST_TILES - 1)
            round_w2(0)
            round_w2(1)
            act.wait_ge(pairs_used, STEPS * PAIR_CHUNKS)
            act.wait_ge(s_copied, TILES)
            for f in range(FIELDS):
                wait(act, s_used, f - S_BUFS + 1)
                nc.scalar.activation(s_hi[:, f % S_BUFS, :], S[:, f, :],
                                     ACT.Copy).then_inc(s_hi_ready, 1)
                if f % W2_FIELDS == 1 and f // W2_FIELDS + 2 < FIELDS // W2_FIELDS:
                    round_w2(f // W2_FIELDS + 2)

            act.wait_ge(mlp_loaded, 7 * 16)
            for m in range(0, HIDDEN1 // P, 2):
                act.wait_ge(h1_made, m + 1)
                nc.scalar.activation(h1[:, m, :], h_ps[m][:, :], ACT.Relu,
                                     bias=bt1_sb[:, m:m + 1]).then_inc(h1_ready[0], 1)
            act.wait_ge(h2_made, 1)
            nc.scalar.activation(h2[:, 0, :], h2_ps[0][:, :], ACT.Relu,
                                 bias=bt2_sb[:, 0:1]).then_inc(h2_ready[0], 1)

        @block.vector
        def _(dve):
            def multiply_pairs(s, par, c):
                width, rows, buf = tiles_of(s) * P, pair_rows(c), c % PAIR_BUFS
                if isinstance(s, int) and s == 0 and c < FIRST_CHUNKS:
                    dve.wait_ge(x0_first_loaded, 2 * 16)
                else:
                    dve.wait_ge(x0_loaded, loads_to(s))
                if c >= PAIR_BUFS:
                    dve.wait_ge(pairs_used, s * PAIR_CHUNKS + c - PAIR_BUFS + 1)
                else:
                    wait(dve, pairs_used, (s - 1) * PAIR_CHUNKS + max(
                        i for i in range(PAIR_CHUNKS) if i % PAIR_BUFS == c) + 1)
                begin = c * GROUPS * P
                nc.vector.tensor_tensor(pairs[0:rows, buf, 0:width], x0_rep[0:rows, 0:width],
                                        x0_shifted[0:rows, begin:begin + width],
                                        ALU.mult).then_inc(pairs_ready, 1)

            def rest_of_pairs(s, c):
                width, rows, buf = tiles_of(s) * P, pair_rows(c), c % PAIR_BUFS
                dve.wait_ge(pairs_hi_ready, split_count(s, c))
                nc.vector.tensor_tensor(pairs_lo[0:rows, buf, 0:width], pairs[0:rows, buf, 0:width],
                                        pairs_hi[0:rows, buf, 0:width],
                                        ALU.subtract).then_inc(pairs_lo_ready, 1)

            def rest_of_x1(s, par):
                width = tiles_of(s) * P
                dve.wait_ge(x1_hi_ready, s + 1)
                nc.vector.tensor_tensor(x1_lo[:, par, 0:width], x1_ps[:, 0:width],
                                        x1_hi[:, par, 0:width], ALU.subtract).then_inc(x1_lo_ready, 1)

            def sum_x1(s, par):
                tiles = tiles_of(s)
                nc.vector.tensor_reduce(
                    r0[:, bass.ds(s * SPS, tiles * SPT)],
                    x1_ps[:, 0:tiles * P].rearrange("p (b d) -> p b d", d=DIM),
                    axis=AX.X, op=ALU.add).then_inc(r0_ready, 1)

            def steps_on(lane, c):
                before = max((i for i in range(c) if V_STEPS[i]), default=None)
                if before is None:
                    return 0
                done = lane + 1 if KIND[before] == MULT_V else lane // 2 + 1
                return V_OPS_TO[before] - V_STEPS[before] + done

            def accumulate(s, par, t, c):
                n, tp = s * GROUPS + t, (par * GROUPS + t) % 2
                if KIND[c] == MULT_V:
                    dve.wait_ge(y_for_vector, n * (Y_CHUNKS - PRODUCTS) + c + 1 - PRODUCTS_TO[c])
                    dve.wait_ge(prod_ready, n * PRODUCTS + PRODUCTS_TO[0])
                    for i in range(chunk_fields(c)):
                        f, lane = c * YF + i, acc_v[:, tp, i * CROSS:(i + 1) * CROSS]
                        if steps_on(i, c):
                            dve.wait_ge(v_op, n * V_OPS + steps_on(i, c))
                        nc.vector.scalar_tensor_tensor(
                            lane, y_bank(c)[:, i * CROSS:(i + 1) * CROSS],
                            x0_rows[:, par, t, f:f + 1], lane, ALU.mult, ALU.add).then_inc(v_op, 1)
                else:
                    dve.wait_ge(prod_ready, n * PRODUCTS + PRODUCTS_TO[c])
                    for begin in (0, 2):
                        end = min(begin + 2, chunk_fields(c))
                        lanes = slice(begin * CROSS, end * CROSS)
                        dve.wait_ge(v_op, n * V_OPS + steps_on(end - 1, c))
                        nc.vector.tensor_tensor(acc_v[:, tp, lanes], acc_v[:, tp, lanes],
                                                prod[:, SLOT[c], lanes], ALU.add).then_inc(v_op, 1)

            def fold(n, tp):
                dve.wait_ge(v_op, (n + 1) * V_OPS)
                nc.vector.tensor_tensor(acc_v[:, tp, 0:2 * CROSS], acc_v[:, tp, 0:2 * CROSS],
                                        acc_v[:, tp, 2 * CROSS:4 * CROSS], ALU.add).then_inc(folded, 1)

            def fold_again(n, tp):
                dve.wait_ge(folded, n * 2 + 1)
                nc.vector.tensor_tensor(acc_v[:, tp, 0:CROSS], acc_v[:, tp, 0:CROSS],
                                        acc_v[:, tp, CROSS:2 * CROSS], ALU.add).then_inc(folded, 1)

            def make_x2(n, tp):
                dve.wait_ge(folded, n * 2 + 2)
                dve.wait_ge(acc_g_ready, n + 1)
                wait(dve, s_made, n - 1)
                nc.vector.tensor_tensor(x2[:, tp, :], acc_v[:, tp, 0:CROSS], acc_g[:, tp, 0:CROSS],
                                        ALU.add).then_inc(x2_ready, 1)

            def step(s, par, pair):
                dve.wait_ge(rows_copied, s + 1)
                for t in range(tiles_of(s)):
                    for c in range(Y_CHUNKS):
                        at = t * Y_CHUNKS + c
                        if KIND[c] in (MULT_V, ADD_V):
                            accumulate(s, par, t, c)
                        n, before = s * GROUPS + t, (par * GROUPS + t + 1) % 2
                        if c == AT_FOLD and (t or not isinstance(s, int) or s):
                            fold_again(n - 1, before)
                        if c == AT_X2 and (t or not isinstance(s, int) or s):
                            make_x2(n - 1, before)
                        if has(s, 1):
                            if at in AT_MULTIPLY:
                                multiply_pairs(s + 1, 1 - par, AT_MULTIPLY.index(at))
                            if at in AT_REST:
                                rest_of_pairs(s + 1, SPLIT_CHUNKS[AT_REST.index(at)])
                            if at == AT_SUM[-1]:
                                rest_of_x1(s + 1, 1 - par)
                            if at == AT_R0:
                                sum_x1(s + 1, 1 - par)
                    fold(n, (par * GROUPS + t) % 2)

            nc.vector.memset(x0_rows[:, :, :, FIELDS:FCOLS], 1.0).then_inc(ones_set, 1)
            dve.wait_ge(w0_loaded, 32)
            nc.vector.tensor_tensor(w0[:, :], w0_raw[0], w0_raw[1], ALU.add).then_inc(w0_ready, 1)
            cols = FIELDS * CROSS // W1_PIECES
            for i in range(W1_PIECES):
                dve.wait_ge(w1_hi_ready, i + 1)
                nc.vector.tensor_tensor(w1_lo[:, i * cols:(i + 1) * cols],
                                        w1_raw[:, i * cols:(i + 1) * cols],
                                        w1_hi[:, i * cols:(i + 1) * cols],
                                        ALU.subtract).then_inc(w1_lo_ready, 1)
            dve.wait_ge(w0_hi_ready, 1)
            nc.vector.tensor_tensor(w0_lo[:, :], w0[:, :], w0_hi[:, :],
                                    ALU.subtract).then_inc(w0_lo_ready, 1)
            for c in range(PAIR_CHUNKS):
                multiply_pairs(0, 0, c)
            rest_of_x1(0, 0)
            sum_x1(0, 0)
            run_steps(dve, step)

            fold_again(TILES - 1, (TILES - 1) % 2)
            make_x2(TILES - 1, (TILES - 1) % 2)
            for f in range(FIELDS):
                dve.wait_ge(s_hi_ready, f + 1)
                nc.vector.tensor_tensor(s_lo[:, f, :], S[:, f, :], s_hi[:, f % S_BUFS, :],
                                        ALU.subtract).then_inc(s_lo_ready, 1)

            dve.wait_ge(r2_made, 1)
            nc.vector.tensor_copy(r2[:, :], r2_ps[:, :]).then_inc(r2_ready, 1)
            dve.wait_ge(mlp_loaded, 7 * 16)
            for m in range(1, HIDDEN1 // P, 2):
                dve.wait_ge(h1_made, m + 1)
                nc.vector.tensor_scalar(h1[:, m, :], h_ps[m][:, :], bt1_sb[:, m:m + 1], 0.0,
                                        ALU.add, ALU.max).then_inc(h1_ready[1], 1)
            dve.wait_ge(h2_made, 2)
            nc.vector.tensor_scalar(h2[:, 1, :], h2_ps[1][:, :], bt2_sb[:, 1:2], 0.0,
                                    ALU.add, ALU.max).then_inc(h2_ready[1], 1)
            dve.wait_ge(y_made, 1)
            nc.vector.tensor_copy(y_sb[:, :], s_ps[0:1, :]).then_inc(y_ready, 1)

        @block.tensor
        def _(pe):
            mm = nc.tensor.matmul

            def transpose_rows(s, par, pair):
                pe.wait_ge(gather_done[par], (pair + 1) * SPT * 16)
                wait(pe, rows_copied, s)
                nc.tensor.transpose(rows_ps[:, 0:GF], gathered[:, par, :],
                                    identity_sb[:, :]).then_inc(transposed, 1)

            def sum_pairs(s, par, c):
                width, rows, i = tiles_of(s) * P, pair_rows(c), s * PAIR_CHUNKS + c
                if c == 0:
                    wait(pe, r0_ready, s)
                out, buf = x1_ps[:, 0:width], c % PAIR_BUFS
                w = slice(c * CROSS, (c + 1) * CROSS)
                first, final = c == 0, c == PAIR_CHUNKS - 1
                if c in SPLIT_CHUNKS and not (isinstance(s, int) and s == 0):
                    pe.wait_ge(pairs_lo_ready, split_count(s, c))
                    hi, lo = pairs_hi[0:rows, buf, 0:width], pairs_lo[0:rows, buf, 0:width]
                    mm(out, w0_hi[0:rows, w], hi, start=first, stop=False)
                    mm(out, w0_lo[0:rows, w], hi, start=False, stop=False)
                    last = mm(out, w0_hi[0:rows, w], lo, start=False, stop=final)
                else:
                    pe.wait_ge(pairs_ready, i + 1)
                    last = mm(out, w0[0:rows, w], pairs[0:rows, buf, 0:width], start=first,
                              stop=final)
                last.then_inc(pairs_used, 1)

            def y_chunk(s, par, t, c):
                n, width = s * GROUPS + t, chunk_fields(c) * CROSS
                if c >= Y_BANKS:
                    wait_chunk_used(pe, c - Y_BANKS, n)
                elif not isinstance(n, int) or n > 0:
                    wait_chunk_used(pe, c + Y_CHUNKS - Y_BANKS, n - 1)
                y = y_bank(c)[:, 0:width]
                w = slice(c * YF * CROSS, c * YF * CROSS + width)
                hi, lo = x1_hi[:, par, t * P:(t + 1) * P], x1_lo[:, par, t * P:(t + 1) * P]
                mm(y, hi, w1_hi[:, w], start=True, stop=False)
                mm(y, hi, w1_lo[:, w], start=False, stop=False)
                mm(y, lo, w1_hi[:, w], start=False, stop=True).then_inc(
                    y_for_vector if KIND[c] == MULT_V else y_for_scalar, 1)

            def make_s(s, par, t):
                n, tp = s * GROUPS + t, (par * GROUPS + t) % 2
                pe.wait_ge(x2_ready, n + 1)
                pe.wait_ge(diag_ready, n + 1)
                wait(pe, s_copied, n)
                mm(s_ps[:, 0:SPT * FCOLS], x2[:, tp, :], x0_diag[:, tp, :],
                   start=True, stop=True).then_inc(s_made, 1)

            def step(s, par, pair):
                pe.wait_ge(x1_hi_ready, s + 1)
                pe.wait_ge(x1_lo_ready, s + 1)
                if isinstance(s, int) and s == 0:
                    pe.wait_ge(w1_lo_ready, W1_PIECES)
                    pe.wait_ge(w0_lo_ready, 1)
                for t in range(tiles_of(s)):
                    for c in range(Y_CHUNKS):
                        at = t * Y_CHUNKS + c
                        y_chunk(s, par, t, c)
                        if has(s, 1):
                            if at == AT_ROWS:
                                transpose_rows(s + 1, 1 - par, pair + par)
                            if at in AT_SUM:
                                sum_pairs(s + 1, 1 - par, AT_SUM.index(at))
                        if c == AT_S:
                            if t > 0:
                                make_s(s, par, t - 1)
                            elif not isinstance(s, int) or s > 0:
                                make_s(s - 1, 1 - par, GROUPS - 1)

            pe.wait_ge(identity_loaded, 16)
            transpose_rows(0, 0, 0)
            for _ in range(WARM_UP):
                mm(s_ps[0:GF, 0:GF], identity_sb[:, :], identity_sb[:, :], start=True, stop=True)
            pe.wait_ge(w0_ready, 1)
            for c in range(PAIR_CHUNKS):
                sum_pairs(0, 0, c)
            run_steps(pe, step)

            def units_of(m):
                return slice(m * P, (m + 1) * P)

            def hidden_before_s(m):
                mm(h_ps[m][:, :], wt1_sb[:, 0, units_of(m)], r0[:, :], start=True, stop=False)
                mm(h_ps[m][:, :], wt1_context_sb[:, units_of(m)], dense_sb[:, :], start=False,
                   stop=False)

            pe.wait_ge(mlp_loaded, 7 * 16)
            pe.wait_ge(r0_ready, STEPS)
            pe.wait_ge(rows_copied, STEPS)
            hidden_before_s(0)
            hidden_before_s(1)
            make_s(STEPS - 1, 1, LAST_TILES - 1)
            pe.wait_ge(prod_ready, TILES * PRODUCTS)
            pe.wait_ge(v_op, TILES * V_OPS)
            hidden_before_s(2)
            hidden_before_s(3)
            pe.wait_ge(s_copied, TILES)
            for m in range(HIDDEN1 // P):
                mm(h_ps[m][:, :], wt1_sb[:, 1, units_of(m)], S[:, FIELDS, :], start=False, stop=False)
            for f in range(FIELDS):
                w = slice(f * CROSS, (f + 1) * CROSS)
                pe.wait_ge(s_lo_ready, f + 1)
                pe.wait_ge(w2_lo_ready, f // W2_FIELDS + 1)
                mm(r2_ps[:, :], w2_hi[:, w], s_hi[:, f % S_BUFS, :], start=f == 0, stop=False)
                mm(r2_ps[:, :], w2_lo[:, w], s_hi[:, f % S_BUFS, :], start=False, stop=False)
                last = mm(r2_ps[:, :], w2_hi[:, w], s_lo[:, f, :],
                          start=False, stop=f == FIELDS - 1)
                last.then_inc(r2_made if f == FIELDS - 1 else s_used, 1)
            pe.wait_ge(r2_ready, 1)
            for m in range(HIDDEN1 // P):
                mm(h_ps[m][:, :], wt1_sb[:, 2, m * P:(m + 1) * P], r2[:, :],
                   start=False, stop=True).then_inc(h1_made, 1)
            for k in range(HIDDEN1 // P):
                pe.wait_ge(h1_ready[k % 2], k // 2 + 1)
                for m in range(HIDDEN2 // P):
                    last = mm(h2_ps[m][:, :], wt2_sb[:, k, m * P:(m + 1) * P], h1[:, k, :],
                              start=k == 0, stop=k == HIDDEN1 // P - 1)
                    if k == HIDDEN1 // P - 1:
                        last.then_inc(h2_made, 1)
            for m in range(HIDDEN2 // P):
                pe.wait_ge(h2_ready[m], 1)
                last = mm(s_ps[0:1, :], wt3_sb[:, m:m + 1], h2[:, m, :],
                          start=m == 0, stop=m == HIDDEN2 // P - 1)
            last.then_inc(y_made, 1)


def pair_layout(w0):
    w0 = w0.reshape(FIELDS, FIELDS, CROSS)
    upper = np.zeros((GF, PAIR_CHUNKS, CROSS), np.float32)
    lower = np.zeros((GF, PAIR_CHUNKS, CROSS), np.float32)
    f = np.arange(FIELDS)
    for s in range(SHIFTS):
        j, c = s // PAIR_CHUNKS, s % PAIR_CHUNKS
        rows = slice(j * FIELDS, (j + 1) * FIELDS)
        upper[rows, c] = w0[f, (f + s) % FIELDS]
        if s:
            lower[rows, c] = w0[(f + s) % FIELDS, f]
    return upper.reshape(GF, -1), lower.reshape(GF, -1)


def kernel(**inputs):
    import concourse.bacc as bacc
    from concourse.bass_utils import run_bass_kernel_spmd

    x = {k: np.asarray(v) for k, v in inputs.items()}
    tables = [x[f"tbl_{i}"] for i in range(FIELDS)]
    sizes = [t.shape[0] for t in tables]
    starts = np.concatenate([[0], np.cumsum(sizes)[:-1]]).astype(np.int32)
    ids = np.zeros((STEPS * SPS, FIELDS), np.int32)
    ids[:BATCH] = x["ids"]
    ids = ids.reshape(STEPS, GROUPS, SPT, FIELDS).transpose(1, 3, 0, 2).reshape(GF, STEPS * SPT)
    mask = np.zeros((P, SPT), np.float32)
    mask[np.arange(P), np.arange(P) // DIM] = 1
    upper, lower = pair_layout(x["L0_rec_f0"])

    def by_g(w):
        return w.reshape(FIELDS, CROSS, CROSS).transpose(1, 0, 2)

    wt1 = x["W_top1"]
    arrays = {
        "in_ids": ids,
        "in_offsets": np.tile(starts, GROUPS)[:, None],
        "in_table": np.concatenate(tables, axis=0),
        "in_identity": np.eye(GF, dtype=np.float32),
        "in_mask": mask,
        "in_w0_upper": upper,
        "in_w0_lower": lower,
        "in_w1": by_g(x["L0_rec_f1"]).reshape(P, FIELDS * CROSS),
        "in_w2": by_g(x["L0_rec_f2"]).reshape(P, FIELDS * CROSS),
        "in_dense": x["dense_ctx"].T,
        "in_wt1": wt1[:3 * P].reshape(3, P, HIDDEN1).transpose(1, 0, 2),
        "in_wt1_context": wt1[3 * P:],
        "in_bt1": x["b_top1"].reshape(-1, P).T,
        "in_wt2": x["W_top2"].reshape(-1, P, HIDDEN2).transpose(1, 0, 2),
        "in_bt2": x["b_top2"].reshape(-1, P).T,
        "in_wt3": x["W_top3"].reshape(-1, P).T,
    }
    arrays = {k: np.ascontiguousarray(v) for k, v in arrays.items()}
    nc = bacc.Bacc("TRN2", target_bir_lowering=False, num_devices=1)
    args = [nc.dram_tensor(k, v.shape, mybir.dt.from_np(v.dtype), kind="ExternalInput").ap()
            for k, v in arrays.items()]
    out = nc.dram_tensor("out_y", (1, BATCH), mybir.dt.float32, kind="ExternalOutput").ap()
    program(nc, *args, out)
    r = run_bass_kernel_spmd(nc, [arrays], core_ids=[0])
    return r.results[0]["out_y"].reshape(BATCH, 1)
```
